# Optimizing a Trainium2 kernel written in Bass

```python
import numpy as np
import jax
import jax.numpy as jnp

def _softmax(x, axis=-1):
    return jax.nn.softmax(x, axis=axis)

def _gelu(x):
    return jax.nn.gelu(x, approximate=True)

def _silu(x):
    return jax.nn.silu(x)

def _sigmoid(x):
    return jax.nn.sigmoid(x)

def _layernorm(x, axis=-1, eps=1e-05):
    m = jnp.mean(x, axis=axis, keepdims=True)
    v = jnp.var(x, axis=axis, keepdims=True)
    return (x - m) / jnp.sqrt(v + eps)

def _scatter_add(tgt, idx, src, axis=0):
    return tgt.at[idx].add(src)

def _segment_sum(src, seg, n):
    return jax.ops.segment_sum(src, seg, n)
kernel_name = 'mk_sandwich_d1_jaxref_r4_8b419f'

def setup_inputs(seed: int=0):
    np.random.seed(seed)
    _w = jnp.asarray

    def _L0_attn_setup():
        import jax, jax.numpy as jnp
        import numpy as np
        D_MODEL = 256
        D_STATE = 16
        D_CONV = 4
        EXPAND = 2
        D_INNER = EXPAND * D_MODEL
        DT_RANK = (D_MODEL + 15) // 16
        BATCH, SEQ_LEN = (2, 512)
        LN_EPS = 1e-05

        def _silu(v):
            return v * jax.nn.sigmoid(v)

        def _selective_scan(x, delta, A, B, C, Dp):
            b, L, d_inner = x.shape
            d_state = A.shape[1]
            xT = jnp.swapaxes(x, 0, 1)
            dT = jnp.swapaxes(delta, 0, 1)
            BT = jnp.swapaxes(B, 0, 1)
            CT = jnp.swapaxes(C, 0, 1)

            def step(h, inp):
                x_t, d_t, B_t, C_t = inp
                dA = jnp.exp(d_t[:, :, None] * A[None, :, :])
                h = dA * h + (d_t * x_t)[:, :, None] * B_t[:, None, :]
                y_t = jnp.einsum('bds,bs->bd', h, C_t)
                return (h, y_t)
            h0 = jnp.zeros((b, d_inner, d_state), x.dtype)
            _, yT = jax.lax.scan(step, h0, (xT, dT, BT, CT))
            y = jnp.swapaxes(yT, 0, 1)
            return y + x * Dp[None, None, :]
        if __name__ == '__main__':
            out = reference(**setup_inputs())
            print(out.shape, out.dtype)
        key = jax.random.key(seed)
        ks = jax.random.split(key, 10)
        s = lambda n: 1.0 / np.sqrt(n)
        x = jax.random.normal(ks[0], (BATCH, SEQ_LEN, D_MODEL), dtype=jnp.float32)
        norm_g = jnp.ones((D_MODEL,), jnp.float32)
        norm_b = jnp.zeros((D_MODEL,), jnp.float32)
        in_proj_w = jax.random.normal(ks[1], (2 * D_INNER, D_MODEL), jnp.float32) * s(D_MODEL)
        conv_w = jax.random.normal(ks[2], (D_INNER, D_CONV), jnp.float32) * s(D_CONV)
        conv_b = jax.random.normal(ks[3], (D_INNER,), jnp.float32) * 0.02
        x_proj_w = jax.random.normal(ks[4], (DT_RANK + 2 * D_STATE, D_INNER), jnp.float32) * s(D_INNER)
        dt_proj_w = jax.random.normal(ks[5], (D_INNER, DT_RANK), jnp.float32) * s(DT_RANK)
        dt_proj_b = jax.random.normal(ks[6], (D_INNER,), jnp.float32) * 0.02
        log_A = jnp.broadcast_to(jnp.log(jnp.arange(1, D_STATE + 1, dtype=jnp.float32))[None, :], (D_INNER, D_STATE))
        Dp = jnp.ones((D_INNER,), jnp.float32)
        out_proj_w = jax.random.normal(ks[7], (D_MODEL, D_INNER), jnp.float32) * s(D_INNER)
        return {'x': x, 'norm_g': norm_g, 'norm_b': norm_b, 'in_proj_w': in_proj_w, 'conv_w': conv_w, 'conv_b': conv_b, 'x_proj_w': x_proj_w, 'dt_proj_w': dt_proj_w, 'dt_proj_b': dt_proj_b, 'log_A': log_A, 'Dp': Dp, 'out_proj_w': out_proj_w}
    _L0_attn_in = _L0_attn_setup()

    def _L0_ffn_setup():
        import jax, jax.numpy as jnp
        import numpy as np
        D_MODEL = 256
        NHEAD = 16
        HEAD_DIM = D_MODEL // NHEAD
        FF = 512
        NUM_EXPERTS = 8
        EPS = 1e-05

        def _ln(x, g, b):
            m = x.mean(-1, keepdims=True)
            v = ((x - m) ** 2).mean(-1, keepdims=True)
            return (x - m) / jnp.sqrt(v + EPS) * g + b

        def _attention(src, Wq, bq, Wk, bk, Wv, bv, Wo, bo):
            B, T, d = src.shape
            scale = HEAD_DIM ** (-0.5)
            q = (src @ Wq + bq).reshape(B, T, NHEAD, HEAD_DIM)
            k = (src @ Wk + bk).reshape(B, T, NHEAD, HEAD_DIM)
            v = (src @ Wv + bv).reshape(B, T, NHEAD, HEAD_DIM)
            scores = jnp.einsum('bqhd,bkhd->bhqk', q, k) * scale
            probs = jax.nn.softmax(scores, axis=-1)
            out = jnp.einsum('bhqk,bkhd->bqhd', probs, v).reshape(B, T, d)
            return out @ Wo + bo

        def _moe(x, gW, gb, W1, b1, W2, b2):
            B, T, d = x.shape
            xf = x.reshape(-1, d)
            gates = jax.nn.softmax(xf @ gW + gb, axis=-1)
            top2_scores, top2_idx = jax.lax.top_k(gates, 2)
            w = (jax.nn.one_hot(top2_idx, NUM_EXPERTS, dtype=xf.dtype) * top2_scores[..., None]).sum(1)
            h = jax.nn.relu(jnp.einsum('nd,edf->enf', xf, W1) + b1[:, None, :])
            y = jnp.einsum('enf,efd->end', h, W2) + b2[:, None, :]
            out = jnp.einsum('ne,end->nd', w, y)
            return out.reshape(B, T, d)
        key = jax.random.key(seed)
        ks = jax.random.split(key, 12)
        s = 0.02
        d, f, E = (D_MODEL, FF, NUM_EXPERTS)
        return {'src': jax.random.normal(ks[0], (8, 128, d), dtype=jnp.float32), 'Wq': jax.random.normal(ks[1], (d, d), dtype=jnp.float32) * s, 'bq': jnp.zeros((d,), jnp.float32), 'Wk': jax.random.normal(ks[2], (d, d), dtype=jnp.float32) * s, 'bk': jnp.zeros((d,), jnp.float32), 'Wv': jax.random.normal(ks[3], (d, d), dtype=jnp.float32) * s, 'bv': jnp.zeros((d,), jnp.float32), 'Wo': jax.random.normal(ks[4], (d, d), dtype=jnp.float32) * s, 'bo': jnp.zeros((d,), jnp.float32), 'gW': jax.random.normal(ks[5], (d, E), dtype=jnp.float32) * s, 'gb': jnp.zeros((E,), jnp.float32), 'W1': jax.random.normal(ks[6], (E, d, f), dtype=jnp.float32) * s, 'b1': jnp.zeros((E, f), jnp.float32), 'W2': jax.random.normal(ks[7], (E, f, d), dtype=jnp.float32) * s, 'b2': jnp.zeros((E, d), jnp.float32), 'ln1_g': jnp.ones((d,), jnp.float32), 'ln1_b': jnp.zeros((d,), jnp.float32), 'ln2_g': jnp.ones((d,), jnp.float32), 'ln2_b': jnp.zeros((d,), jnp.float32)}
    _L0_ffn_in = _L0_ffn_setup()
    _d = {'L0_attn_x': _L0_attn_in['x'], 'L0_attn_norm_g': _L0_attn_in['norm_g'], 'L0_attn_norm_b': _L0_attn_in['norm_b'], 'L0_attn_in_proj_w': _L0_attn_in['in_proj_w'], 'L0_attn_conv_w': _L0_attn_in['conv_w'], 'L0_attn_conv_b': _L0_attn_in['conv_b'], 'L0_attn_x_proj_w': _L0_attn_in['x_proj_w'], 'L0_attn_dt_proj_w': _L0_attn_in['dt_proj_w'], 'L0_attn_dt_proj_b': _L0_attn_in['dt_proj_b'], 'L0_attn_log_A': _L0_attn_in['log_A'], 'L0_attn_Dp': _L0_attn_in['Dp'], 'L0_attn_out_proj_w': _L0_attn_in['out_proj_w'], 'L0_ffn_Wq': _L0_ffn_in['Wq'], 'L0_ffn_bq': _L0_ffn_in['bq'], 'L0_ffn_Wk': _L0_ffn_in['Wk'], 'L0_ffn_bk': _L0_ffn_in['bk'], 'L0_ffn_Wv': _L0_ffn_in['Wv'], 'L0_ffn_bv': _L0_ffn_in['bv'], 'L0_ffn_Wo': _L0_ffn_in['Wo'], 'L0_ffn_bo': _L0_ffn_in['bo'], 'L0_ffn_gW': _L0_ffn_in['gW'], 'L0_ffn_gb': _L0_ffn_in['gb'], 'L0_ffn_W1': _L0_ffn_in['W1'], 'L0_ffn_b1': _L0_ffn_in['b1'], 'L0_ffn_W2': _L0_ffn_in['W2'], 'L0_ffn_b2': _L0_ffn_in['b2'], 'L0_ffn_ln1_g': _L0_ffn_in['ln1_g'], 'L0_ffn_ln1_b': _L0_ffn_in['ln1_b'], 'L0_ffn_ln2_g': _L0_ffn_in['ln2_g'], 'L0_ffn_ln2_b': _L0_ffn_in['ln2_b']}
    _x0 = _d['L0_attn_x']
    _d['L0_attn_x'] = jax.random.normal(jax.random.fold_in(jax.random.key(seed), 1), (1, 4096, 256), dtype=_x0.dtype)
    del _x0
    return _d

def reference(L0_attn_x, L0_attn_norm_g, L0_attn_norm_b, L0_attn_in_proj_w, L0_attn_conv_w, L0_attn_conv_b, L0_attn_x_proj_w, L0_attn_dt_proj_w, L0_attn_dt_proj_b, L0_attn_log_A, L0_attn_Dp, L0_attn_out_proj_w, L0_ffn_Wq, L0_ffn_bq, L0_ffn_Wk, L0_ffn_bk, L0_ffn_Wv, L0_ffn_bv, L0_ffn_Wo, L0_ffn_bo, L0_ffn_gW, L0_ffn_gb, L0_ffn_W1, L0_ffn_b1, L0_ffn_W2, L0_ffn_b2, L0_ffn_ln1_g, L0_ffn_ln1_b, L0_ffn_ln2_g, L0_ffn_ln2_b):

    def _L0_attn_ref(x, norm_g, norm_b, in_proj_w, conv_w, conv_b, x_proj_w, dt_proj_w, dt_proj_b, log_A, Dp, out_proj_w):
        import jax, jax.numpy as jnp
        import numpy as np
        D_MODEL = 256
        D_STATE = 16
        D_CONV = 4
        EXPAND = 2
        D_INNER = EXPAND * D_MODEL
        DT_RANK = (D_MODEL + 15) // 16
        BATCH, SEQ_LEN = (2, 512)
        LN_EPS = 1e-05

        def _silu(v):
            return v * jax.nn.sigmoid(v)

        def _selective_scan(x, delta, A, B, C, Dp):
            b, L, d_inner = x.shape
            d_state = A.shape[1]
            xT = jnp.swapaxes(x, 0, 1)
            dT = jnp.swapaxes(delta, 0, 1)
            BT = jnp.swapaxes(B, 0, 1)
            CT = jnp.swapaxes(C, 0, 1)

            def step(h, inp):
                x_t, d_t, B_t, C_t = inp
                dA = jnp.exp(d_t[:, :, None] * A[None, :, :])
                h = dA * h + (d_t * x_t)[:, :, None] * B_t[:, None, :]
                y_t = jnp.einsum('bds,bs->bd', h, C_t)
                return (h, y_t)
            h0 = jnp.zeros((b, d_inner, d_state), x.dtype)
            _, yT = jax.lax.scan(step, h0, (xT, dT, BT, CT))
            y = jnp.swapaxes(yT, 0, 1)
            return y + x * Dp[None, None, :]
        if __name__ == '__main__':
            out = reference(**setup_inputs())
            print(out.shape, out.dtype)
        residual = x
        mu = jnp.mean(x, axis=-1, keepdims=True)
        var = jnp.mean((x - mu) ** 2, axis=-1, keepdims=True)
        xn = (x - mu) * jax.lax.rsqrt(var + LN_EPS) * norm_g + norm_b
        xz = jnp.einsum('bld,ed->ble', xn, in_proj_w)
        x_ssm, z = jnp.split(xz, 2, axis=-1)
        L = x.shape[1]
        xpad = jnp.pad(x_ssm, ((0, 0), (D_CONV - 1, 0), (0, 0)))
        conv = sum((xpad[:, k:k + L, :] * conv_w[None, None, :, k] for k in range(D_CONV))) + conv_b
        x_ssm = _silu(conv)
        xp = jnp.einsum('bld,ed->ble', x_ssm, x_proj_w)
        dt, B, C = jnp.split(xp, [DT_RANK, DT_RANK + D_STATE], axis=-1)
        delta = jax.nn.softplus(jnp.einsum('blr,dr->bld', dt, dt_proj_w) + dt_proj_b)
        A = -jnp.exp(log_A)
        y = _selective_scan(x_ssm, delta, A, B, C, Dp)
        y = y * _silu(z)
        out = jnp.einsum('ble,de->bld', y, out_proj_w)
        return out + residual

    def _L0_ffn_ref(src, Wq, bq, Wk, bk, Wv, bv, Wo, bo, gW, gb, W1, b1, W2, b2, ln1_g, ln1_b, ln2_g, ln2_b):
        import jax, jax.numpy as jnp
        import numpy as np
        D_MODEL = 256
        NHEAD = 16
        HEAD_DIM = D_MODEL // NHEAD
        FF = 512
        NUM_EXPERTS = 8
        EPS = 1e-05

        def _ln(x, g, b):
            m = x.mean(-1, keepdims=True)
            v = ((x - m) ** 2).mean(-1, keepdims=True)
            return (x - m) / jnp.sqrt(v + EPS) * g + b

        def _attention(src, Wq, bq, Wk, bk, Wv, bv, Wo, bo):
            B, T, d = src.shape
            scale = HEAD_DIM ** (-0.5)
            q = (src @ Wq + bq).reshape(B, T, NHEAD, HEAD_DIM)
            k = (src @ Wk + bk).reshape(B, T, NHEAD, HEAD_DIM)
            v = (src @ Wv + bv).reshape(B, T, NHEAD, HEAD_DIM)
            scores = jnp.einsum('bqhd,bkhd->bhqk', q, k) * scale
            probs = jax.nn.softmax(scores, axis=-1)
            out = jnp.einsum('bhqk,bkhd->bqhd', probs, v).reshape(B, T, d)
            return out @ Wo + bo

        def _moe(x, gW, gb, W1, b1, W2, b2):
            B, T, d = x.shape
            xf = x.reshape(-1, d)
            gates = jax.nn.softmax(xf @ gW + gb, axis=-1)
            top2_scores, top2_idx = jax.lax.top_k(gates, 2)
            w = (jax.nn.one_hot(top2_idx, NUM_EXPERTS, dtype=xf.dtype) * top2_scores[..., None]).sum(1)
            h = jax.nn.relu(jnp.einsum('nd,edf->enf', xf, W1) + b1[:, None, :])
            y = jnp.einsum('enf,efd->end', h, W2) + b2[:, None, :]
            out = jnp.einsum('ne,end->nd', w, y)
            return out.reshape(B, T, d)
        attn_out = _attention(src, Wq, bq, Wk, bk, Wv, bv, Wo, bo)
        x = _ln(src + attn_out, ln1_g, ln1_b)
        ff = _moe(x, gW, gb, W1, b1, W2, b2)
        return _ln(x + ff, ln2_g, ln2_b)
    x = L0_attn_x
    x = x + _layernorm(_L0_attn_ref(_layernorm(x, axis=-1), L0_attn_norm_g, L0_attn_norm_b, L0_attn_in_proj_w, L0_attn_conv_w, L0_attn_conv_b, L0_attn_x_proj_w, L0_attn_dt_proj_w, L0_attn_dt_proj_b, L0_attn_log_A, L0_attn_Dp, L0_attn_out_proj_w), axis=-1)
    x = x + _layernorm(_L0_ffn_ref(_layernorm(x, axis=-1), L0_ffn_Wq, L0_ffn_bq, L0_ffn_Wk, L0_ffn_bk, L0_ffn_Wv, L0_ffn_bv, L0_ffn_Wo, L0_ffn_bo, L0_ffn_gW, L0_ffn_gb, L0_ffn_W1, L0_ffn_b1, L0_ffn_W2, L0_ffn_b2, L0_ffn_ln1_g, L0_ffn_ln1_b, L0_ffn_ln2_g, L0_ffn_ln2_b), axis=-1)
    return x

_drawn_inputs = setup_inputs


def setup_inputs(seed=0):
    import zlib

    import numpy as np

    out = dict(_drawn_inputs(seed))
    spreads = {'L0_attn_norm_g': (1.0, 0.2),
     'L0_attn_norm_b': (0.0, 0.1),
     'L0_attn_Dp': (1.0, 0.2),
     'L0_ffn_bq': (0.0, 0.8),
     'L0_ffn_bk': (0.0, 0.8),
     'L0_ffn_bv': (0.0, 0.795),
     'L0_ffn_bo': (0.0, 0.1),
     'L0_ffn_gb': (0.0, 0.8),
     'L0_ffn_b1': (0.0, 0.8),
     'L0_ffn_b2': (0.0, 0.8),
     'L0_ffn_ln1_g': (1.0, 0.2),
     'L0_ffn_ln1_b': (0.0, 0.1),
     'L0_ffn_ln2_g': (1.0, 0.2),
     'L0_ffn_ln2_b': (0.0, 0.1)}
    factors = {'L0_attn_conv_b': 6.753,
     'L0_attn_dt_proj_b': 8.0,
     'L0_ffn_Wq': 8.0,
     'L0_ffn_Wk': 8.0,
     'L0_ffn_Wv': 8.0,
     'L0_ffn_Wo': 5.354,
     'L0_ffn_gW': 5.108,
     'L0_ffn_W1': 7.495,
     'L0_ffn_W2': 6.008}
    for name, (base, spread) in spreads.items():
        noise = np.random.default_rng([zlib.crc32(name.encode()), seed]).standard_normal(out[name].shape)
        drawn = base * np.exp(spread * noise) if base else spread * noise
        out[name] = jnp.asarray(drawn.astype(out[name].dtype))
    for name, factor in factors.items():
        out[name] = (out[name] * factor).astype(out[name].dtype)
    return out
```

```python
from contextlib import ExitStack

import numpy as np

import concourse.bass as bass
from concourse import mybir

F32 = mybir.dt.float32
BF16 = mybir.dt.bfloat16
ALU = mybir.AluOpType
ACT = mybir.ActivationFunctionType
X = mybir.AxisListType.X

P = 128
T = 4096
D = 256
KT = D // P
CH = 512
NCH = T // CH
TT = CH // P
DI = 512
CT = DI // P
NS = 16
R = 16
TAPS = 4
XP = R + 2 * NS
H = 16
HD = D // H
NE = 8
FF = 512
FT = FF // P
EPS = 1e-5
TERMS = 6
KR = TERMS * HD
SPLITS = 3
VW = 32
NB = H * NCH
NT = T // P
UNITS = NT // 2


class Scratch:

    def __init__(self, nc):
        self.x1 = nc.dram_tensor("x1_scratch", (T, D), F32).ap()
        self.src = nc.dram_tensor("src_scratch", (T, D), F32).ap()
        self.v = nc.dram_tensor("v_scratch", (T, D), F32).ap()
        self.q = nc.dram_tensor("q_scratch", (SPLITS, D, T), BF16).ap()
        self.k = nc.dram_tensor("k_scratch", (SPLITS, D, T), BF16).ap()
        self.attn = nc.dram_tensor("attn_scratch", (T, D), F32).ap()


def settled(engine, sem, value):
    engine.wait_ge(sem, value)


def inverse_deviations(nc, pool, sems, n, mv, powers, met):
    _, var_ready, rstd_ready, rstd, eps_added = sems
    settled(pool, *met)
    pool.wait_ge(var_ready, n)
    nc.gpsimd.tensor_tensor(rstd[:, :], mv[:, :, 1], powers[:, 0, :], ALU.add).then_inc(eps_added, 1)
    settled(pool, *met)
    pool.wait_ge(eps_added, n)
    nc.gpsimd.tensor_tensor(rstd[:, :], rstd[:, :], powers[:, 1, :], ALU.pow).then_inc(rstd_ready, 1)


def layernorm(nc, dve, src, dst, stats, mv, sems, n, done, value):
    stats_done, var_ready, rstd_ready, rstd, _ = sems
    for t in range(TT):
        last = nc.vector.bn_stats(stats[:, t, :], src(t))
    last.then_inc(stats_done, 1)
    dve.wait_ge(stats_done, n)
    nc.vector.memset(rstd[:, 0:1], 0.0)
    for t in range(TT):
        last = nc.vector.bn_aggr(mv[:, t, :], stats[:, t, :])
    last.then_inc(var_ready, 1)
    dve.wait_ge(rstd_ready, n)
    for t in range(TT):
        last = nc.vector.tensor_scalar(dst(t), src(t), mv[:, t, 0:1], rstd[:, t:t + 1], ALU.subtract, ALU.mult)
    last.then_inc(done, 1)
    dve.wait_ge(done, value)


def token_rows(dram, chunk):
    rows = dram[chunk * CH:(chunk + 1) * CH, :] if type(chunk) is int else dram[bass.ds(chunk * CH, CH), :]
    return rows.rearrange("(t p) d -> p t d", p=P)


def mamba_stage(nc, a, scr):
    ctx, stage = ExitStack(), "mamba"
    with ctx:
        def sb(name, shape, dt=F32):
            return ctx.enter_context(nc.sbuf_tensor(f"{stage}_{name}", shape, dt))

        def sem(name):
            return ctx.enter_context(nc.semaphore(f"{stage}_{name}"))

        ident = sb("ident", [P, P])
        w_in = sb("w_in", [P, KT, 2 * DI])
        w_xp = sb("w_xp", [P, CT, XP])
        w_dt = sb("w_dt", [R, DI])
        w_out = sb("w_out", [P, CT, D])
        w_qkv = sb("w_qkv", [P, KT, 3, D])
        conv_w = sb("conv_w", [P, CT, TAPS])
        conv_b = sb("conv_b", [P, CT])
        dt_b = sb("dt_b", [P, CT])
        d_skip = sb("d_skip", [P, CT])
        a_neg = sb("a_neg", [P, CT, NS])
        norm_g = sb("norm_g", [P, KT])
        norm_b = sb("norm_b", [P, KT])
        qk_b = sb("qk_b", [P, 4])
        bv_rows = sb("bv_rows", [P, D])
        conv_diag = sb("conv_diag", [P, CT, TAPS, P])
        skip_diag = sb("skip_diag", [P, CT, P])
        select = sb("select", [XP, 2 * NS, P], BF16)
        xin = sb("xin", [P, 2, TT, D])
        xn0 = sb("xn0", [P, TT, D])
        xm = sb("xm", [P, TT, D])
        xmT = sb("xmT", [P, KT, CH])
        xs = sb("xs", [P, CT, TAPS - 1 + CH])
        zs = sb("zs", [P, CT, CH])
        xc = sb("xc", [P, CT, CH])
        xp = sb("xp", [XP, CH])
        xp_parts = sb("xp_parts", [XP, SPLITS, CH], BF16)
        soft = sb("soft", [P, CT, CH])
        delta = sb("delta", [P, CT, CH])
        dx = sb("dx", [P, CT, CH])
        dA = sb("dA", [P, 2, CT, CH])
        dBx = sb("dBx", [P, CT, CH])
        hs = sb("hs", [P, 2, CT, CH])
        c_rows = sb("c_rows", [P, 2, CH])
        hc = sb("hc", [P, 2, CT, CH])
        carry = sb("carry", [P, NS, CT])
        x1c = sb("x1c", [P, TT, D])
        srcc = sb("srcc", [P, TT, D])
        vc = sb("vc", [P, TT, D])
        qk_parts = sb("qk_parts", [P, SPLITS, 4, CH], BF16)
        yg = soft
        qk = dBx
        srcT = xmT
        stats = sb("stats", [P, TT, 6])
        mv = sb("mv", [P, TT, 2])
        rstd = sb("rstd", [P, TT])
        powers = sb("powers", [P, 2, TT])
        table_warm = sb("table_warm", [P, 1])
        bank = ctx.enter_context(nc.psum_tensor("m_bank", [P, 8, CH], F32))

        (weights_in, x_in, consts_zero, consts_set, signs, diags, xm_ready, xmT_ps, xmT_ready, inproj_ps, halo_done,
         xs_ready, zs_ready, conv_ps, xc_ready, xp_ps, xp_ready, parts_ready, dt_ps, abs_done, exp_done,
         soft_ready, delta_ready, dx_ready, bc_ps, dA_ready, c_ready, dBx_ready, scan_done, carry_done,
         hc_ready, y_added, yg_ready, mo_ps, src_ready, srcT_ps, srcT_ready, qk_ps, qk_biased, qk_hi,
         qk_rest, qk_mid, qk_parts_ready, v_ps, v_ready, stored, xn0_ready, mo_ready,
         mo_normal, x1_ready, stats_done, var_ready, rstd_ready, eps_added) = [sem(n) for n in (
             "weights_in x_in consts_zero consts_set signs diags xm_ready xmT_ps xmT_ready inproj_ps halo_done "
             "xs_ready zs_ready conv_ps xc_ready xp_ps xp_ready parts_ready dt_ps abs_done exp_done "
             "soft_ready delta_ready dx_ready bc_ps dA_ready c_ready dBx_ready scan_done carry_done "
             "hc_ready y_added yg_ready mo_ps src_ready srcT_ps srcT_ready qk_ps qk_biased qk_hi "
             "qk_rest qk_mid qk_parts_ready v_ps v_ready stored xn0_ready mo_ready "
             "mo_normal x1_ready stats_done var_ready rstd_ready eps_added").split()]
        STORES = 3 + 2 * SPLITS * 2
        ln_sems = stats_done, var_ready, rstd_ready, rstd, eps_added
        block = ctx.enter_context(nc.Block())

        loads = [
            (w_in[:, :, :], a["in_w"].rearrange("(k p) n -> p k n", p=P)),
            (w_xp[:, :, :], a["xp_w"].rearrange("(k p) n -> p k n", p=P)),
            (w_dt[:, :], a["dt_w"]),
            (w_out[:, :, :], a["out_w"].rearrange("(k p) n -> p k n", p=P)),
            (w_qkv[:, :, 0, :], a["Wq"].rearrange("(k p) n -> p k n", p=P)),
            (w_qkv[:, :, 1, :], a["Wk"].rearrange("(k p) n -> p k n", p=P)),
            (w_qkv[:, :, 2, :], a["Wv"].rearrange("(k p) n -> p k n", p=P)),
            (conv_w[:, :, :], a["conv_w"].rearrange("(c p) k -> p c k", p=P)),
            (a_neg[:, :, :], a["log_A"].rearrange("(c p) s -> p c s", p=P)),
            (conv_b[:, :], a["conv_b"]),
            (dt_b[:, :], a["dt_b"]),
            (d_skip[:, :], a["Dp"]),
            (norm_g[:, :], a["norm_g"]),
            (norm_b[:, :], a["norm_b"]),
            (qk_b[:, 0:2], a["bq"]),
            (qk_b[:, 2:4], a["bk"]),
            (bv_rows[:, :], a["bv"].rearrange("(o d) -> o d", o=1).broadcast_to((P, D))),
        ]

        met = weights_in, 16 * len(loads)

        @block.sync
        def _(sp):
            sp.dma_start(xin[:, 0, :, :], token_rows(a["x"], 0)).then_inc(x_in, 16)
            for dst, src in loads:
                sp.dma_start(dst, src).then_inc(weights_in, 16)
            sp.wait_ge(x_in, 16)
            sp.dma_start(xin[:, 1, :, :], token_rows(a["x"], 1)).then_inc(x_in, 16)
            with sp.Fori(0, NCH) as c:
                settled(sp, *met)
                sp.wait_ge(src_ready, c + 1)
                settled(sp, *met)
                sp.wait_ge(x_in, 16 * (c + 2))
                sp.dma_start(xin[:, bass.ds(c % 2, 1), :, :].rearrange("p o t d -> p (o t) d"),
                             token_rows(a["x"], (c + 2) % NCH)).then_inc(x_in, 16)
                sp.dma_start(token_rows(scr.x1, c), x1c[:, :, :]).then_inc(stored, 16)
                sp.dma_start(token_rows(scr.src, c), srcc[:, :, :]).then_inc(stored, 16)
                settled(sp, *met)
                sp.wait_ge(v_ready, c + 1)
                sp.dma_start(token_rows(scr.v, c), vc[:, :, :]).then_inc(stored, 16)
                settled(sp, *met)
                sp.wait_ge(qk_parts_ready, c + 1)
                for n in range(SPLITS):
                    for i, dram in ((0, scr.q), (1, scr.k)):
                        for j in range(2):
                            sp.dma_start(dram[n, j * P:(j + 1) * P, bass.ds(c * CH, CH)],
                                         qk_parts[:, n, 2 * i + j, :]).then_inc(stored, 16)
            sp.wait_ge(x_in, 16 * (NCH + 2))
            sp.wait_ge(stored, 16 * (STORES * NCH + 1))

        @block.gpsimd
        def _(pool):
            nc.gpsimd.memset(ident[:, :], 0.0).then_inc(consts_zero, 1)
            nc.gpsimd.memset(select[:, :, :], 0.0).then_inc(consts_zero, 1)
            pool.wait_ge(consts_zero, 2)
            nc.gpsimd.affine_select(out=ident[:, :], in_=ident[:, :], compare_op=ALU.not_equal, fill=1.0,
                                    base=0, pattern=[[-1, P]], channel_multiplier=1).then_inc(consts_set, 1)
            nc.gpsimd.affine_select(out=select[:, :, :], in_=select[:, :, :], compare_op=ALU.not_equal, fill=1.0,
                                    base=-R, pattern=[[-1, 2 * NS], [0, P]], channel_multiplier=1).then_inc(consts_set, 1)
            nc.gpsimd.memset(carry[:, :, :], 0.0).then_inc(consts_set, 1)
            nc.gpsimd.memset(powers[:, 0, :], EPS).then_inc(consts_set, 1)
            nc.gpsimd.memset(powers[:, 1, :], -0.5).then_inc(consts_set, 1)
            pool.wait_ge(consts_set, 5)
            pool.sem_inc(hc_ready, 2)
            pool.sem_inc(y_added, 2)
            pool.sem_inc(scan_done, 2 * CT)
            pool.sem_inc(dBx_ready, 1)
            pool.sem_inc(c_ready, 1)
            pool.sem_inc(qk_biased, 4)
            pool.sem_inc(stored, 16)
            with pool.Fori(0, NCH) as c:
                for n in range(2):
                    inverse_deviations(nc, pool, ln_sems, 4 * c + n + 1, mv, powers, met)
                with pool.Fori(0, NS) as s:
                    u = c * NS + s
                    pool.wait_ge(c_ready, u + 2)
                    pool.wait_ge(scan_done, (u + 3) * CT)
                    pool.wait_ge(y_added, u + 1)
                    h_par = hs[:, bass.ds(u % 2, 1), :, :].rearrange("p o c t -> p (o c) t")
                    hc_par = hc[:, bass.ds(u % 2, 1), :, :].rearrange("p o c t -> p (o c) t")
                    nc.gpsimd.tensor_tensor(hc_par, h_par, c_rows[:, bass.ds(u % 2, 1), :].broadcast_to((P, CT, CH)),
                                            ALU.mult).then_inc(hc_ready, 1)
                for n in range(2, 4):
                    inverse_deviations(nc, pool, ln_sems, 4 * c + n + 1, mv, powers, met)

        @block.vector
        def _(dve):
            dve.wait_ge(consts_set, 5)
            nc.vector.memset(xs[:, :, :], 0.0).then_inc(diags, 1)
            dve.wait_ge(weights_in, 16 * len(loads))
            for ct in range(CT):
                for k in range(TAPS):
                    nc.vector.tensor_scalar(conv_diag[:, ct, k, :], ident[:, :], conv_w[:, ct, k:k + 1], None,
                                            ALU.mult).then_inc(diags, 1)
                nc.vector.tensor_scalar(skip_diag[:, ct, :], ident[:, :], d_skip[:, ct:ct + 1], None,
                                        ALU.mult).then_inc(diags, 1)
            dve.wait_ge(signs, 1)
            nc.vector.tensor_scalar(a_neg[:, :, :], a_neg[:, :, :], -1.0, None, ALU.mult).then_inc(diags, 1)
            dve.wait_ge(diags, CT * (TAPS + 1) + 2)
            with dve.Fori(0, NCH) as c:
                dve.wait_ge(x_in, 16 * (c + 1))
                xc_in = xin[:, bass.ds(c % 2, 1), :, :].rearrange("p o t d -> p (o t) d")
                layernorm(nc, dve, lambda t: xc_in[:, t, :], lambda t: xn0[:, t, :], stats, mv, ln_sems, 4 * c + 1, xn0_ready, c + 1)
                layernorm(nc, dve, lambda t: xn0[:, t, :], lambda t: xm[:, t, :], stats, mv, ln_sems, 4 * c + 2, xm_ready, c + 1)
                nc.vector.tensor_copy(xs[:, :, 0:TAPS - 1], xs[:, :, CH:CH + TAPS - 1]).then_inc(halo_done, 1)
                dve.wait_ge(halo_done, c + 1)
                for j in range(CT):
                    dve.wait_ge(inproj_ps, 2 * CT * c + j + 1)
                    nc.vector.tensor_copy(xs[:, j, TAPS - 1:], bank[:, 2 + j, :]).then_inc(xs_ready, 1)
                dve.wait_ge(xp_ps, c + 1)
                nc.vector.tensor_copy(xp[:, :], bank[0:XP, 6, :]).then_inc(xp_ready, 1)
                dve.wait_ge(xp_ready, 4 * c + 1)
                nc.vector.tensor_copy(xp_parts[:, 0, :], xp[:, :]).then_inc(xp_ready, 1)
                dve.wait_ge(xp_ready, 4 * c + 2)
                nc.vector.tensor_tensor(qk[0:XP, 0, :], xp[:, :], xp_parts[:, 0, :], ALU.subtract).then_inc(xp_ready, 1)
                dve.wait_ge(xp_ready, 4 * c + 3)
                nc.vector.tensor_copy(xp_parts[:, 1, :], qk[0:XP, 0, :]).then_inc(xp_ready, 1)
                dve.wait_ge(xp_ready, 4 * c + 4)
                nc.vector.tensor_tensor(xp_parts[:, 2, :], qk[0:XP, 0, :], xp_parts[:, 1, :],
                                        ALU.subtract).then_inc(parts_ready, 1)
                dve.wait_ge(soft_ready, c + 1)
                nc.vector.tensor_tensor(delta[:, :, :], delta[:, :, :], soft[:, :, :], ALU.add).then_inc(delta_ready, 1)
                dve.wait_ge(delta_ready, c + 1)
                nc.vector.tensor_tensor(dx[:, :, :], delta[:, :, :], xc[:, :, :], ALU.mult).then_inc(dx_ready, 1)
                settled(dve, *met)
                dve.wait_ge(dx_ready, c + 1)
                with dve.Fori(0, NS) as s:
                    u = c * NS + s
                    dve.wait_ge(bc_ps, u + 1)
                    b_row = bank[:, bass.ds(4 + u % 2, 1), :].broadcast_to((P, CT, CH))
                    nc.vector.tensor_tensor(dBx[:, :, :], dx[:, :, :], b_row, ALU.mult).then_inc(dBx_ready, 1)
                    dve.wait_ge(dA_ready, (u + 1) * CT)
                    dve.wait_ge(hc_ready, u + 1)
                    dve.wait_ge(dBx_ready, u + 2)
                    for ct in range(CT):
                        nc.vector.tensor_tensor_scan(
                            hs[:, bass.ds(u % 2, 1), ct, :].rearrange("p o t -> p (o t)"),
                            dA[:, bass.ds(u % 2, 1), ct, :].rearrange("p o t -> p (o t)"), dBx[:, ct, :],
                            carry[:, bass.ds(s, 1), ct], ALU.mult, ALU.add).then_inc(scan_done, 1)
                    dve.wait_ge(scan_done, (u + 3) * CT)
                    nc.vector.tensor_copy(carry[:, bass.ds(s, 1), :].rearrange("p o c -> p (o c)"),
                                          hs[:, bass.ds(u % 2, 1), :, CH - 1].rearrange("p o c -> p (o c)")
                                          ).then_inc(carry_done, 1)
                dve.wait_ge(carry_done, NS * (c + 1))
                dve.wait_ge(y_added, NS * (c + 1) + 2)
                nc.vector.tensor_tensor(yg[:, :, :], bank[:, 0:CT, :], zs[:, :, :], ALU.mult).then_inc(yg_ready, 1)
                dve.wait_ge(mo_ps, c + 1)
                mo = bank[:, 4:6, :].rearrange("p b (h d) -> p (b h) d", d=D)
                nc.vector.tensor_tensor(xm[:, :, :], mo, xn0[:, :, :], ALU.add).then_inc(mo_ready, 1)
                dve.wait_ge(mo_ready, c + 1)
                layernorm(nc, dve, lambda t: xm[:, t, :], lambda t: xm[:, t, :], stats, mv, ln_sems, 4 * c + 3, mo_normal, c + 1)
                dve.wait_ge(stored, 16 * (STORES * c + 1))
                nc.vector.tensor_tensor(x1c[:, :, :], xm[:, :, :], xc_in, ALU.add).then_inc(x1_ready, 1)
                dve.wait_ge(x1_ready, c + 1)
                layernorm(nc, dve, lambda t: x1c[:, t, :], lambda t: srcc[:, t, :], stats, mv, ln_sems, 4 * c + 4, src_ready, c + 1)
                dve.wait_ge(qk_hi, c + 1)
                nc.vector.tensor_tensor(qk[:, :, :], qk[:, :, :], qk_parts[:, 0, :, :], ALU.subtract).then_inc(qk_rest, 1)
                dve.wait_ge(v_ps, c + 1)
                nc.vector.tensor_tensor(vc[:, :, :], mo, bv_rows[:, :].rearrange("p (o d) -> p o d", o=1)
                                        .broadcast_to((P, TT, D)), ALU.add).then_inc(v_ready, 1)
                dve.wait_ge(qk_mid, c + 1)
                nc.vector.tensor_tensor(qk_parts[:, 2, :, :], qk[:, :, :], qk_parts[:, 1, :, :],
                                        ALU.subtract).then_inc(qk_parts_ready, 1)
                dve.wait_ge(qk_parts_ready, c + 1)

        @block.scalar
        def _(act):
            act.wait_ge(weights_in, 16 * len(loads))
            nc.scalar.activation(a_neg[:, :, :], a_neg[:, :, :], ACT.Exp).then_inc(signs, 1)
            act.wait_ge(diags, CT * (TAPS + 1) + 2)
            with act.Fori(0, NCH) as c:
                act.wait_ge(xmT_ps, c + 1)
                for k in range(KT):
                    nc.scalar.activation(xmT[:, k, :], bank[:, k, :], ACT.Identity, bias=norm_b[:, k:k + 1],
                                         scale=norm_g[:, k:k + 1]).then_inc(xmT_ready, 1)
                for j in range(CT):
                    act.wait_ge(inproj_ps, 2 * CT * c + CT + j + 1)
                    nc.scalar.activation(zs[:, j, :], bank[:, (6 + j) % 8, :], ACT.Silu).then_inc(zs_ready, 1)
                for j in range(CT):
                    act.wait_ge(conv_ps, CT * c + j + 1)
                    nc.scalar.activation(xc[:, j, :], bank[:, 2 + j, :], ACT.Silu,
                                         bias=conv_b[:, j:j + 1]).then_inc(xc_ready, 1)
                for j in range(CT):
                    act.wait_ge(dt_ps, CT * c + j + 1)
                    nc.scalar.activation(soft[:, j, :], bank[:, j, :], ACT.Abs, bias=dt_b[:, j:j + 1]).then_inc(abs_done, 1)
                    nc.scalar.activation(delta[:, j, :], bank[:, j, :], ACT.Relu, bias=dt_b[:, j:j + 1]).then_inc(abs_done, 1)
                act.wait_ge(abs_done, 2 * CT * (c + 1))
                nc.scalar.activation(soft[:, :, :], soft[:, :, :], ACT.Exp, scale=-1.0).then_inc(exp_done, 1)
                act.wait_ge(exp_done, 2 * c + 1)
                nc.scalar.activation(soft[:, :, :], soft[:, :, :], ACT.Ln, bias=1.0).then_inc(soft_ready, 1)
                act.wait_ge(delta_ready, c + 1)
                nc.scalar.activation(table_warm[:, :], conv_b[:, 0:1], ACT.Exp, scale=0.0).then_inc(exp_done, 1)
                act.wait_ge(exp_done, 2 * c + 2)
                with act.Fori(0, NS) as s:
                    u = c * NS + s
                    act.wait_ge(scan_done, (u + 1) * CT)
                    for ct in range(CT):
                        nc.scalar.activation(dA[:, bass.ds(u % 2, 1), ct, :].rearrange("p o t -> p (o t)"),
                                             delta[:, ct, :], ACT.Exp,
                                             scale=a_neg[:, ct, bass.ds(s, 1)]).then_inc(dA_ready, 1)
                    act.wait_ge(bc_ps, u + 1)
                    act.wait_ge(hc_ready, u + 1)
                    nc.scalar.activation(c_rows[:, bass.ds(u % 2, 1), :], bank[:, bass.ds(6 + u % 2, 1), :],
                                         ACT.Copy).then_inc(c_ready, 1)
                act.wait_ge(srcT_ps, c + 1)
                nc.scalar.activation(srcT[:, :, :], bank[:, 0:KT, :], ACT.Copy).then_inc(srcT_ready, 1)
                for i, b in enumerate((2, 3, 6, 7)):
                    act.wait_ge(qk_ps, 4 * c + i + 1)
                    nc.scalar.activation(qk[:, i, :], bank[:, b, :], ACT.Identity, bias=qk_b[:, i:i + 1]
                                         ).then_inc(qk_biased, 1)
                act.wait_ge(qk_biased, 4 * (c + 2))
                nc.scalar.activation(qk_parts[:, 0, :, :], qk[:, :, :], ACT.Copy).then_inc(qk_hi, 1)
                act.wait_ge(qk_rest, c + 1)
                nc.scalar.activation(qk_parts[:, 1, :, :], qk[:, :, :], ACT.Copy).then_inc(qk_mid, 1)

        @block.tensor
        def _(pe):
            pe.wait_ge(diags, CT * (TAPS + 1) + 2)
            with pe.Fori(0, NCH) as c:
                def transposed(src, done):
                    for k in range(KT):
                        for t in range(TT):
                            last = nc.tensor.transpose(bank[:, k, t * P:(t + 1) * P], src[:, t, k * P:(k + 1) * P],
                                                       ident[:, :])
                    last.then_inc(done, 1)

                pe.wait_ge(xm_ready, c + 1)
                pe.wait_ge(qk_biased, 4 * (c + 1))
                transposed(xm, xmT_ps)
                pe.wait_ge(xmT_ready, KT * (c + 1))
                for j in range(2 * CT):
                    for k in range(KT):
                        last = nc.tensor.matmul(bank[:, (2 + j) % 8, :], w_in[:, k, j * P:(j + 1) * P], xmT[:, k, :],
                                                start=k == 0, stop=k == KT - 1)
                    last.then_inc(inproj_ps, 1)
                for j in range(CT):
                    pe.wait_ge(xs_ready, CT * c + j + 1)
                    for k in range(TAPS):
                        last = nc.tensor.matmul(bank[:, 2 + j, :], conv_diag[:, j, k, :], xs[:, j, k:k + CH],
                                                start=k == 0, stop=k == TAPS - 1)
                    last.then_inc(conv_ps, 1)
                pe.wait_ge(zs_ready, CT * (c + 1))
                for j in range(CT):
                    pe.wait_ge(xc_ready, CT * c + j + 1)
                    last = nc.tensor.matmul(bank[0:XP, 6, :], w_xp[:, j, :], xc[:, j, :], start=j == 0, stop=j == CT - 1)
                last.then_inc(xp_ps, 1)
                pe.wait_ge(xp_ready, 4 * c + 1)
                for j in range(CT):
                    nc.tensor.matmul(bank[:, j, :], w_dt[:, j * P:(j + 1) * P], xp[0:R, :],
                                     start=True, stop=True).then_inc(dt_ps, 1)
                pe.wait_ge(parts_ready, c + 1)

                def state_rows(u, s):
                    for i in range(2):
                        for n in range(SPLITS):
                            last = nc.tensor.matmul(
                                bank[:, bass.ds(4 + 2 * i + u % 2, 1), :].rearrange("p o t -> p (o t)"),
                                select[:, bass.ds(i * NS + s, 1), :].rearrange("r o p -> r (o p)"), xp_parts[:, n, :],
                                start=n == 0, stop=n == SPLITS - 1)
                    last.then_inc(bc_ps, 1)

                def add_state(u):
                    pe.wait_ge(hc_ready, u + 3)
                    for ct in range(CT):
                        last = nc.tensor.matmul(bank[:, ct, :], ident[:, :],
                                                hc[:, bass.ds(u % 2, 1), ct, :].rearrange("p o t -> p (o t)"),
                                                start=False, stop=True, skip_group_check=True)
                    last.then_inc(y_added, 1)

                u0 = c * NS
                state_rows(u0, 0)
                pe.wait_ge(delta_ready, c + 1)
                for ct in range(CT):
                    nc.tensor.matmul(bank[:, ct, :], skip_diag[:, ct, :], xc[:, ct, :], start=True, stop=True,
                                     skip_group_check=True)
                with pe.Fori(0, NS - 1) as s:
                    u = c * NS + s
                    pe.wait_ge(dBx_ready, u + 1)
                    pe.wait_ge(c_ready, u + 1)
                    state_rows(u + 1, s + 1)
                    add_state(u)
                add_state(u0 + NS - 1)
                pe.wait_ge(yg_ready, c + 1)
                for t in range(TT):
                    for ct in range(CT):
                        last = nc.tensor.matmul(bank[:, 4 + t // 2, (t % 2) * D:(t % 2 + 1) * D],
                                                yg[:, ct, t * P:(t + 1) * P], w_out[:, ct, :],
                                                start=ct == 0, stop=ct == CT - 1)
                last.then_inc(mo_ps, 1)
                pe.wait_ge(src_ready, c + 1)
                transposed(srcc, srcT_ps)
                pe.wait_ge(srcT_ready, c + 1)
                for i, b in enumerate((2, 3, 6, 7)):
                    for k in range(KT):
                        last = nc.tensor.matmul(bank[:, b, :], w_qkv[:, k, i // 2, (i % 2) * P:(i % 2 + 1) * P],
                                                srcT[:, k, :], start=k == 0, stop=k == KT - 1)
                    last.then_inc(qk_ps, 1)
                for t in range(TT):
                    for k in range(KT):
                        last = nc.tensor.matmul(bank[:, 4 + t // 2, (t % 2) * D:(t % 2 + 1) * D],
                                                srcT[:, k, t * P:(t + 1) * P], w_qkv[:, k, 2, :],
                                                start=k == 0, stop=k == KT - 1)
                last.then_inc(v_ps, 1)


MAX_JOBS = TT * NCH
MAX_PER_UNIT = [3, 2] * 6 + [2] + [0] * (UNITS - 13)
assert sum(MAX_PER_UNIT) == MAX_JOBS
NP = 4


def attention_stage(nc, a, scr):
    ctx, stage = ExitStack(), "attention"
    with ctx:
        def sb(name, shape, dt=F32):
            return ctx.enter_context(nc.sbuf_tensor(f"{stage}_{name}", shape, dt))

        def sem(name):
            return ctx.enter_context(nc.semaphore(f"{stage}_{name}"))

        qst = sb("qst", [P, 2 * T], BF16)
        kst = sb("kst", [P, 2 * T], BF16)
        vtok = sb("vtok", [P, NT, D])
        vh = sb("vh", [P, NT, VW])
        probs = sb("probs", [P, NP, 2, CH])
        oT = sb("oT", [P, CH])
        attn = sb("attn", [P, NT, D])
        identb = sb("identb", [P, P], BF16)
        gather = sb("gather", [P, HD + 1])
        mx = sb("mx", [P, TT, NCH])
        neg_max = sb("neg_max", [P, TT])
        max_parts = sb("max_parts", [P, TT, SPLITS], BF16)
        sums = sb("sums", [P, TT])
        table_warm = sb("table_warm", [P, 1])
        bank = ctx.enter_context(nc.psum_tensor(f"{stage}_bank", [P, 8, CH], F32))
        SCORES, MAXES, OUT, SMALL = 0, 4, 6, 7

        (zeroed, consts, q_in, v_in, heads_in, vh_ready, scored, exp_done, pv_done, max_scored, max_done, negated,
         parts_done, max_rows, rows_ready, oT_ready, summed, inverted, normal, stored) = [sem(n) for n in (
             "zeroed consts q_in v_in heads_in vh_ready scored exp_done pv_done max_scored max_done negated "
             "parts_done max_rows rows_ready oT_ready summed inverted normal stored").split()]
        HEAD_LOADS = 2 * TERMS
        block = ctx.enter_context(nc.Block())

        def ring(b):
            return (b % (2 * NCH)) * CH

        def load_head(sp, h, half):
            rows = bass.ds(h * HD, HD)
            cols = slice(half * T, (half + 1) * T) if type(half) is int else bass.ds(half * T, T)
            for i, n in enumerate((0, 0, 0, 1, 1, 2)):
                sp.dma_start(qst[i * HD:(i + 1) * HD, cols], scr.q[n, rows, :]).then_inc(heads_in, 16)
            for i, n in ((0, 3), (3, 2), (5, 1)):
                for j in range(n):
                    sp.dma_start(kst[(i + j) * HD:(i + j + 1) * HD, cols], scr.k[j, rows, :]).then_inc(heads_in, 16)

        @block.sync
        def _(sp):
            sp.wait_ge(consts, 1)
            load_head(sp, 0, 0)
            sp.dma_start(vtok[:, :, :], scr.v.rearrange("(t p) d -> p t d", p=P)).then_inc(v_in, 16)
            sp.wait_ge(heads_in, 16 * HEAD_LOADS)
            load_head(sp, 1, 1)
            with sp.Fori(2, H) as h:
                sp.wait_ge(heads_in, 16 * HEAD_LOADS * h)
                settled(sp, consts, 1)
                sp.wait_ge(pv_done, NCH * (h - 1) * UNITS)
                load_head(sp, h, h % 2)
            sp.wait_ge(heads_in, 16 * HEAD_LOADS * H)
            sp.wait_ge(normal, NB)
            sp.dma_start(scr.attn.rearrange("(t p) d -> p t d", p=P), attn[:, :, :]).then_inc(stored, 16)
            sp.wait_ge(stored, 16)

        @block.gpsimd
        def _(pool):
            nc.gpsimd.memset(kst[96:128, :], 1.0).then_inc(consts, 1)
            pool.wait_ge(consts, 1)
            nc.gpsimd.memset(identb[:, :], 0.0).then_inc(zeroed, 1)
            nc.gpsimd.memset(gather[:, :], 0.0).then_inc(zeroed, 1)
            nc.gpsimd.memset(vh[:, :, :], 0.0).then_inc(zeroed, 1)
            pool.wait_ge(zeroed, 3)
            nc.gpsimd.memset(vh[:, :, HD:HD + 1], 1.0).then_inc(consts, 1)
            nc.gpsimd.affine_select(out=identb[:, :], in_=identb[:, :], compare_op=ALU.not_equal, fill=1.0,
                                    base=0, pattern=[[-1, P]], channel_multiplier=1).then_inc(consts, 1)
            for j in range(P // VW):
                nc.gpsimd.affine_select(out=gather[:, :], in_=gather[:, :], compare_op=ALU.not_equal, fill=1.0,
                                        base=-VW * j, pattern=[[-1, HD + 1]], channel_multiplier=1).then_inc(consts, 1)
                pool.wait_ge(consts, 4 + j)
            pool.wait_ge(v_in, 16)
            pool.sem_inc(summed, 1)
            nc.gpsimd.tensor_copy(vh[:, :, 0:HD], vtok[:, :, 0:HD]).then_inc(vh_ready, 1)
            with pool.Fori(1, H) as h:
                pool.wait_ge(pv_done, NCH * h * UNITS)
                settled(pool, v_in, 16)
                nc.gpsimd.tensor_copy(vh[:, :, 0:HD], vtok[:, :, bass.ds(h * HD, HD)]).then_inc(vh_ready, 1)

        CONSTS = 3 + P // VW

        @block.scalar
        def _(act):
            act.wait_ge(consts, CONSTS)
            nc.scalar.activation(table_warm[:, :], gather[:, 0:1], ACT.Exp).then_inc(zeroed, 1)

            def take_sums(b):
                act.wait_ge(pv_done, (b + 1) * UNITS)
                act.wait_ge(summed, b + 1)
                nc.scalar.activation(oT[:, :], bank[:, OUT, :], ACT.Copy).then_inc(oT_ready, 1)

            def exponentials(b, first):
                for u in range(UNITS):
                    act.wait_ge(scored, b * UNITS + u + 1)
                    if not (first and u < NP):
                        act.wait_ge(pv_done, b * UNITS + u - NP + 1)
                    nc.scalar.activation(probs[:, u % NP, :, :], bank[:, SCORES + 2 * (u % 2):SCORES + 2 * (u % 2) + 2, :],
                                         ACT.Exp, scale=float(HD) ** -0.5).then_inc(exp_done, 1)
                    if u == 0 and not first:
                        take_sums(b - 1)

            exponentials(0, True)
            with act.Fori(1, NB) as b:
                exponentials(b, False)
            take_sums(NB - 1)

        @block.vector
        def _(dve):
            dve.wait_ge(consts, CONSTS)

            def normalise(b):
                small = bank[:, SMALL, 0:TT * VW].rearrange("p (t w) -> p t w", w=VW)
                dve.wait_ge(summed, b + 2)
                nc.vector.reciprocal(sums[:, :], small[:, :, HD]).then_inc(inverted, 1)
                dve.wait_ge(inverted, b + 1)
                tiles = slice(b % NCH * TT, b % NCH * TT + TT) if type(b) is int else bass.ds(b % NCH * TT, TT)
                head = slice(b // NCH * HD, b // NCH * HD + HD) if type(b) is int else bass.ds(b // NCH * HD, HD)
                nc.vector.tensor_tensor(attn[:, tiles, head], small[:, :, 0:HD],
                                        sums[:, :].rearrange("p (t o) -> p t o", o=1).broadcast_to((P, TT, HD)),
                                        ALU.mult).then_inc(normal, 1)

            def maxima(b, normal_of=None):
                n = 0
                for u in range(UNITS):
                    if u == 4 and normal_of is not None:
                        normalise(normal_of)
                    for _ in range(MAX_PER_UNIT[u]):
                        dve.wait_ge(max_scored, b * MAX_JOBS + n + 1)
                        nc.vector.reduce_max(mx[:, n // NCH, n % NCH:n % NCH + 1], bank[:, MAXES + n % 2, :], X
                                             ).then_inc(max_done, 1)
                        n += 1
                dve.wait_ge(max_done, (b + 1) * MAX_JOBS)
                nc.vector.tensor_reduce(neg_max[:, :], mx[:, :, :], X, ALU.max, negate=True).then_inc(negated, 1)
                dve.wait_ge(negated, b + 1)
                nc.vector.tensor_copy(max_parts[:, :, 0], neg_max[:, :]).then_inc(parts_done, 1)
                dve.wait_ge(parts_done, 5 * b + 1)
                nc.vector.tensor_tensor(neg_max[:, :], neg_max[:, :], max_parts[:, :, 0], ALU.subtract).then_inc(parts_done, 1)
                dve.wait_ge(parts_done, 5 * b + 2)
                nc.vector.tensor_copy(max_parts[:, :, 1], neg_max[:, :]).then_inc(parts_done, 1)
                dve.wait_ge(parts_done, 5 * b + 3)
                nc.vector.tensor_tensor(neg_max[:, :], neg_max[:, :], max_parts[:, :, 1], ALU.subtract).then_inc(parts_done, 1)
                dve.wait_ge(parts_done, 5 * b + 4)
                nc.vector.tensor_copy(max_parts[:, :, 2], neg_max[:, :]).then_inc(parts_done, 1)
                dve.wait_ge(max_rows, b + 1)
                cols = slice(ring(b), ring(b) + CH) if type(b) is int else bass.ds(ring(b), CH)
                nc.vector.tensor_copy(qst[KR:KR + SPLITS, cols], bank[KR:KR + SPLITS, SMALL, :]).then_inc(rows_ready, 1)

            maxima(0)
            maxima(1)
            with dve.Fori(2, NB) as b:
                maxima(b, b - 2)
            normalise(NB - 2)
            normalise(NB - 1)

        @block.tensor
        def _(pe):
            pe.wait_ge(consts, CONSTS)

            def columns(start, n):
                return slice(start, start + n) if type(start) is int else bass.ds(start, n)

            def score_unit(b, u):
                if u >= 2:
                    pe.wait_ge(exp_done, b * UNITS + u - 1)
                for i in range(2):
                    last = nc.tensor.matmul(bank[:, SCORES + 2 * (u % 2) + i, :],
                                            kst[0:KR + SPLITS, columns(b // NCH % 2 * T + (2 * u + i) * P, P)],
                                            qst[0:KR + SPLITS, columns(ring(b), CH)], start=True, stop=True)
                last.then_inc(scored, 1)

            def max_jobs(b, n0, count, first):
                for n in range(n0, n0 + count):
                    if not (first and n < 2):
                        pe.wait_ge(max_done, b * MAX_JOBS + n - 1)
                    nc.tensor.matmul(bank[:, MAXES + n % 2, :],
                                     qst[0:KR, columns(ring(b) + n // NCH * P, P)],
                                     kst[0:KR, columns(b // NCH % 2 * T + n % NCH * CH, CH)],
                                     start=True, stop=True).then_inc(max_scored, 1)

            def max_to_rows(b):
                pe.wait_ge(parts_done, 5 * (b + 1))
                for t in range(TT):
                    last = nc.tensor.matmul(bank[KR:KR + SPLITS, SMALL, t * P:(t + 1) * P], max_parts[:, t, :],
                                            identb[:, :], start=True, stop=True)
                last.then_inc(max_rows, 1)

            def value_unit(b, u):
                pe.wait_ge(exp_done, b * UNITS + u + 1)
                for i in range(2):
                    kt = 2 * u + i
                    g = kt % 4
                    last = nc.tensor.matmul(bank[VW * g:VW * (g + 1), OUT, :], vh[:, kt, :], probs[:, u % NP, i, :],
                                            start=kt < 4, stop=kt >= NT - 4)
                last.then_inc(pv_done, 1)

            def add_groups(b):
                pe.wait_ge(oT_ready, b + 1)
                for t in range(TT):
                    last = nc.tensor.matmul(bank[:, SMALL, t * VW:t * VW + HD + 1], oT[:, t * P:(t + 1) * P],
                                            gather[:, :], start=True, stop=True)
                last.then_inc(summed, 1)

            def one_block(b, first, last):
                if not last:
                    pe.wait_ge(heads_in, ((b + 1) // NCH + 1) * 16 * HEAD_LOADS)
                pe.wait_ge(rows_ready, b + 1)
                score_unit(b, 0)
                n = 0
                for u in range(UNITS):
                    if u + 1 < UNITS:
                        score_unit(b, u + 1)
                    if not last:
                        max_jobs(b + 1, n, MAX_PER_UNIT[u], False)
                        n += MAX_PER_UNIT[u]
                    if u == 0:
                        pe.wait_ge(vh_ready, b // NCH + 1)
                        if not first:
                            pe.wait_ge(oT_ready, b)
                    value_unit(b, u)
                    if u == 1 and not first:
                        add_groups(b - 1)
                    if u == UNITS - 2 and not last:
                        if not first:
                            pe.wait_ge(normal, b)
                        max_to_rows(b + 1)

            pe.wait_ge(heads_in, 16 * HEAD_LOADS)
            max_jobs(0, 0, MAX_JOBS, True)
            max_to_rows(0)
            one_block(0, True, False)
            with pe.Fori(1, NB - 1) as b:
                one_block(b, False, False)
            one_block(NB - 1, False, True)
            pe.wait_ge(normal, NB - 1)
            add_groups(NB - 1)


def expert_stage(nc, a, scr, out):
    ctx, stage = ExitStack(), "experts"
    with ctx:
        def sb(name, shape, dt=F32):
            return ctx.enter_context(nc.sbuf_tensor(f"{stage}_{name}", shape, dt))

        def sem(name):
            return ctx.enter_context(nc.semaphore(f"{stage}_{name}"))

        w1 = sb("w1", [P, KT, NE, FF])
        w2 = sb("w2", [P, NE, FT, D])
        wo = sb("wo", [P, KT, D])
        gw = sb("gw", [P, KT, NE])
        b1 = sb("b1", [P, NE * FT])
        b2 = sb("b2", [NE, D])
        rows = {n: sb(n + "_rows", [P, D]) for n in ("bo", "ln1_g", "ln1_b", "ln2_g", "ln2_b")}
        gb_rows = sb("gb_rows", [P, NE])
        ident = sb("ident", [P, P])
        before = sb("before", [P, NE, NE])
        powers = sb("powers", [P, 2, TT])
        table_warm = sb("table_warm", [P, 1])
        at_in = sb("at_in", [P, TT, D])
        src_in = sb("src_in", [P, TT, D])
        x1_in = sb("x1_in", [P, TT, D])
        atT = sb("atT", [P, KT, CH])
        xa = sb("xa", [P, TT, D])
        xn = sb("xn", [P, TT, D])
        xaT = sb("xaT", [P, KT, CH])
        hT = sb("hT", [P, 2, FT, CH])
        acc = sb("acc", [P, TT, D])
        outc = sb("outc", [P, TT, D])
        logits = sb("logits", [P, TT, NE])
        gates = sb("gates", [P, TT, NE])
        top = sb("top", [P, TT])
        over = sb("over", [P, TT, NE, NE])
        ties = sb("ties", [P, TT, NE, NE])
        rank = sb("rank", [P, TT, NE])
        weights = sb("weights", [P, TT, NE])
        wT = sb("wT", [NE, CH])
        stats = sb("stats", [P, TT, 6])
        mv = sb("mv", [P, TT, 2])
        rstd = sb("rstd", [P, TT])
        bank = ctx.enter_context(nc.psum_tensor(f"{stage}_bank", [P, 8, CH], F32))

        (weights_in, at_loaded, src_loaded, x1_loaded, zeroed, consts, atT_ps, atT_ready, wo_ps, added, src_used,
         normal1, xa_ready, xaT_ps, xaT_ready, gates_ps, gate_steps, shifted, exp_done, weights_ready, wT_ps, wT_ready,
         bias_ps, h_ps, h_ready, y_ps, y_added, x2_ready, normal2, out_ready, stored, stats_done, var_ready,
         rstd_ready, eps_added, moe_normal) = [sem(n) for n in (
             "weights_in at_loaded src_loaded x1_loaded zeroed consts atT_ps atT_ready wo_ps added src_used "
             "normal1 xa_ready xaT_ps xaT_ready gates_ps gate_steps shifted exp_done weights_ready wT_ps wT_ready "
             "bias_ps h_ps h_ready y_ps y_added x2_ready normal2 out_ready stored stats_done var_ready "
             "rstd_ready eps_added moe_normal").split()]
        ln_sems = stats_done, var_ready, rstd_ready, rstd, eps_added
        block = ctx.enter_context(nc.Block())

        def to_rows(name, width):
            return a[name].rearrange("(o d) -> o d", o=1).broadcast_to((P, width))

        loads = [
            (wo[:, :, :], a["Wo"].rearrange("(k p) n -> p k n", p=P)),
            (gw[:, :, :], a["gW"].rearrange("(k p) n -> p k n", p=P)),
            (b1[:, :], a["b1"]),
            (b2[:, :], a["b2"]),
            (gb_rows[:, :], to_rows("gb", NE)),
            *[(r[:, :], to_rows(n, D)) for n, r in rows.items()],
            *[(w1[:, k, :, :], a["W1"][:, k * P:(k + 1) * P, :].rearrange("e p f -> p e f")) for k in range(KT)],
            *[(w2[:, e, :, :], a["W2"][e, :, :].rearrange("(f p) d -> p f d", p=P)) for e in range(NE)],
        ]
        met = weights_in, 16 * len(loads)

        @block.sync
        def _(sp):
            sp.dma_start(at_in[:, :, :], token_rows(scr.attn, 0)).then_inc(at_loaded, 16)
            sp.dma_start(src_in[:, :, :], token_rows(scr.src, 0)).then_inc(src_loaded, 16)
            sp.dma_start(x1_in[:, :, :], token_rows(scr.x1, 0)).then_inc(x1_loaded, 16)
            for dst, src in loads:
                sp.dma_start(dst, src).then_inc(weights_in, 16)
            sp.wait_ge(*met)
            with sp.Fori(0, NCH) as c:
                settled(sp, *met)
                sp.wait_ge(atT_ps, c + 1)
                sp.dma_start(at_in[:, :, :], token_rows(scr.attn, (c + 1) % NCH)).then_inc(at_loaded, 16)
                settled(sp, *met)
                sp.wait_ge(src_used, c + 1)
                sp.dma_start(src_in[:, :, :], token_rows(scr.src, (c + 1) % NCH)).then_inc(src_loaded, 16)
                settled(sp, *met)
                sp.wait_ge(out_ready, c + 1)
                sp.dma_start(x1_in[:, :, :], token_rows(scr.x1, (c + 1) % NCH)).then_inc(x1_loaded, 16)
                sp.dma_start(token_rows(out, c), outc[:, :, :]).then_inc(stored, 16)
            sp.wait_ge(at_loaded, 16 * (NCH + 1))
            sp.wait_ge(src_loaded, 16 * (NCH + 1))
            sp.wait_ge(x1_loaded, 16 * (NCH + 1))
            sp.wait_ge(stored, 16 * (NCH + 1))

        @block.gpsimd
        def _(pool):
            nc.gpsimd.memset(ident[:, :], 0.0).then_inc(zeroed, 1)
            nc.gpsimd.memset(before[:, :, :], 1.0).then_inc(zeroed, 1)
            nc.gpsimd.memset(powers[:, 0, :], EPS).then_inc(zeroed, 1)
            nc.gpsimd.memset(powers[:, 1, :], -0.5).then_inc(zeroed, 1)
            pool.wait_ge(zeroed, 4)
            nc.gpsimd.affine_select(out=ident[:, :], in_=ident[:, :], compare_op=ALU.not_equal, fill=1.0,
                                    base=0, pattern=[[-1, P]], channel_multiplier=1).then_inc(consts, 1)
            nc.gpsimd.affine_select(out=before[:, :, :], in_=before[:, :, :], compare_op=ALU.is_gt, fill=0.0,
                                    base=0, pattern=[[1, NE], [-1, NE]], channel_multiplier=0).then_inc(consts, 1)
            pool.wait_ge(*met)
            pool.sem_inc(y_added, 1)
            pool.sem_inc(stored, 16)
            with pool.Fori(0, NCH) as c:
                for n in range(3):
                    inverse_deviations(nc, pool, ln_sems, 3 * c + n + 1, mv, powers, met)

        @block.scalar
        def _(act):
            act.wait_ge(consts, 2)
            act.wait_ge(*met)
            nc.scalar.activation(table_warm[:, :], ident[:, 0:1], ACT.Exp).then_inc(zeroed, 1)
            with act.Fori(0, NCH) as c:
                act.wait_ge(atT_ps, c + 1)
                nc.scalar.activation(atT[:, :, :], bank[:, 0:KT, :], ACT.Copy).then_inc(atT_ready, 1)
                act.wait_ge(xaT_ps, c + 1)
                nc.scalar.activation(xaT[:, :, :], bank[:, 0:KT, :], ACT.Copy).then_inc(xaT_ready, 1)
                act.wait_ge(shifted, c + 1)
                nc.scalar.activation(gates[:, :, :], logits[:, :, :], ACT.Exp).then_inc(exp_done, 1)
                act.wait_ge(wT_ps, c + 1)
                nc.scalar.activation(wT[:, :], bank[0:NE, 3, :], ACT.Copy).then_inc(wT_ready, 1)
                for e in range(NE):
                    if e >= 2:
                        act.wait_ge(y_ps, c * NE + e - 1)
                    for f in range(FT):
                        act.wait_ge(h_ps, (c * NE + e) * FT + f + 1)
                        nc.scalar.activation(hT[:, e % 2, f, :], bank[:, 2 + f, :], ACT.Relu,
                                             bias=b1[:, e * FT + f:e * FT + f + 1]).then_inc(h_ready, 1)

        @block.vector
        def _(dve):
            dve.wait_ge(consts, 2)
            dve.wait_ge(*met)

            def over_tiles(v):
                return v[:, :].rearrange("p (o d) -> p o d", o=1).broadcast_to((P, TT, v.shape[-1]))

            def halves(first):
                return bank[:, first:first + 2, :].rearrange("p b (h d) -> p (b h) d", d=D)

            with dve.Fori(0, NCH) as c:
                dve.wait_ge(wo_ps, c + 1)
                nc.vector.tensor_tensor(xa[:, :, :], halves(2), over_tiles(rows["bo"]), ALU.add).then_inc(added, 1)
                dve.wait_ge(src_loaded, 16 * (c + 1))
                dve.wait_ge(added, 4 * c + 1)
                nc.vector.tensor_tensor(xa[:, :, :], xa[:, :, :], src_in[:, :, :], ALU.add).then_inc(src_used, 1)
                dve.wait_ge(src_used, c + 1)
                layernorm(nc, dve, lambda t: xa[:, t, :], lambda t: xn[:, t, :], stats, mv, ln_sems, 3 * c + 1, normal1, c + 1)
                nc.vector.tensor_tensor(xn[:, :, :], xn[:, :, :], over_tiles(rows["ln1_g"]), ALU.mult).then_inc(added, 1)
                dve.wait_ge(added, 4 * c + 2)
                nc.vector.tensor_tensor(xa[:, :, :], xn[:, :, :], over_tiles(rows["ln1_b"]), ALU.add).then_inc(xa_ready, 1)
                base = 9 * c
                dve.wait_ge(gates_ps, c + 1)
                pl = bank[:, 2, 0:TT * NE].rearrange("p (t e) -> p t e", e=NE)
                nc.vector.tensor_tensor(logits[:, :, :], pl, over_tiles(gb_rows), ALU.add).then_inc(gate_steps, 1)
                dve.wait_ge(gate_steps, base + 1)
                nc.vector.reduce_max(top[:, :], logits[:, :, :], X).then_inc(gate_steps, 1)
                dve.wait_ge(gate_steps, base + 2)

                def per_token(v):
                    return v[:, :].rearrange("p (t o) -> p t o", o=1).broadcast_to((P, TT, NE))

                nc.vector.tensor_tensor(logits[:, :, :], logits[:, :, :], per_token(top), ALU.subtract).then_inc(shifted, 1)
                dve.wait_ge(exp_done, c + 1)
                nc.vector.reduce_sum(top[:, :], gates[:, :, :], X).then_inc(gate_steps, 1)
                dve.wait_ge(gate_steps, base + 3)
                nc.vector.reciprocal(top[:, :], top[:, :]).then_inc(gate_steps, 1)
                dve.wait_ge(gate_steps, base + 4)
                nc.vector.tensor_tensor(gates[:, :, :], gates[:, :, :], per_token(top), ALU.mult).then_inc(gate_steps, 1)
                dve.wait_ge(gate_steps, base + 5)
                others = [gates[:, :, :].rearrange("p t (o j) -> p t o j", o=1).broadcast_to((P, TT, NE, NE))[:, t, :, :]
                          for t in range(TT)]
                own = [gates[:, :, :].rearrange("p t (e o) -> p t e o", o=1).broadcast_to((P, TT, NE, NE))[:, t, :, :]
                       for t in range(TT)]
                for t in range(TT):
                    nc.vector.tensor_tensor(over[:, t, :, :], others[t], own[t], ALU.is_gt)
                    last = nc.vector.tensor_tensor(ties[:, t, :, :], others[t], own[t], ALU.is_equal)
                last.then_inc(gate_steps, 1)
                dve.wait_ge(gate_steps, base + 6)
                for t in range(TT):
                    last = nc.vector.tensor_tensor(ties[:, t, :, :], ties[:, t, :, :], before[:, :, :], ALU.mult)
                last.then_inc(gate_steps, 1)
                dve.wait_ge(gate_steps, base + 7)
                nc.vector.tensor_tensor(over[:, :, :, :], over[:, :, :, :], ties[:, :, :, :], ALU.add).then_inc(gate_steps, 1)
                dve.wait_ge(gate_steps, base + 8)
                nc.vector.reduce_sum(rank[:, :, :], over[:, :, :, :], X).then_inc(gate_steps, 1)
                dve.wait_ge(gate_steps, base + 9)
                nc.vector.scalar_tensor_tensor(weights[:, :, :], rank[:, :, :], 1.5, gates[:, :, :], ALU.is_lt, ALU.mult
                                               ).then_inc(weights_ready, 1)
                dve.wait_ge(bias_ps, c + 1)
                nc.vector.tensor_copy(acc[:, :, :], halves(0)).then_inc(added, 1)
                dve.wait_ge(added, 4 * c + 3)
                for e in range(NE):
                    dve.wait_ge(y_ps, c * NE + e + 1)
                    y = halves(6)
                    for t in range(TT):
                        last = nc.vector.scalar_tensor_tensor(acc[:, t, :], y[:, t, :], weights[:, t, e:e + 1], acc[:, t, :],
                                                              ALU.mult, ALU.add)
                    last.then_inc(y_added, 1)
                    dve.wait_ge(y_added, c * NE + e + 2)
                nc.vector.tensor_tensor(acc[:, :, :], acc[:, :, :], xa[:, :, :], ALU.add).then_inc(x2_ready, 1)
                dve.wait_ge(x2_ready, c + 1)
                layernorm(nc, dve, lambda t: acc[:, t, :], lambda t: xn[:, t, :], stats, mv, ln_sems, 3 * c + 2, normal2, 2 * c + 1)
                nc.vector.tensor_tensor(xn[:, :, :], xn[:, :, :], over_tiles(rows["ln2_g"]), ALU.mult).then_inc(added, 1)
                dve.wait_ge(added, 4 * c + 4)
                nc.vector.tensor_tensor(acc[:, :, :], xn[:, :, :], over_tiles(rows["ln2_b"]), ALU.add).then_inc(moe_normal, 1)
                dve.wait_ge(moe_normal, c + 1)
                layernorm(nc, dve, lambda t: acc[:, t, :], lambda t: xn[:, t, :], stats, mv, ln_sems, 3 * c + 3, normal2, 2 * c + 2)
                dve.wait_ge(x1_loaded, 16 * (c + 1))
                dve.wait_ge(stored, 16 * (c + 1))
                nc.vector.tensor_tensor(outc[:, :, :], xn[:, :, :], x1_in[:, :, :], ALU.add).then_inc(out_ready, 1)

        @block.tensor
        def _(pe):
            pe.wait_ge(consts, 2)
            pe.wait_ge(*met)

            def transposed(src, done):
                for k in range(KT):
                    for t in range(TT):
                        last = nc.tensor.transpose(bank[:, k, t * P:(t + 1) * P], src[:, t, k * P:(k + 1) * P], ident[:, :])
                last.then_inc(done, 1)

            def by_tokens(first, lhsT, rhs, n, done):
                for t in range(TT):
                    for k in range(n):
                        last = nc.tensor.matmul(bank[:, first + t // 2, (t % 2) * D:(t % 2 + 1) * D], lhsT(k, t), rhs(k),
                                                start=k == 0, stop=k == n - 1)
                last.then_inc(done, 1)

            with pe.Fori(0, NCH) as c:
                pe.wait_ge(at_loaded, 16 * (c + 1))
                transposed(at_in, atT_ps)
                pe.wait_ge(atT_ready, c + 1)
                by_tokens(2, lambda k, t: atT[:, k, t * P:(t + 1) * P], lambda k: wo[:, k, :], KT, wo_ps)
                pe.wait_ge(xa_ready, c + 1)
                transposed(xa, xaT_ps)
                pe.wait_ge(xaT_ready, c + 1)
                for t in range(TT):
                    for k in range(KT):
                        last = nc.tensor.matmul(bank[:, 2, t * NE:(t + 1) * NE], xaT[:, k, t * P:(t + 1) * P], gw[:, k, :],
                                                start=k == 0, stop=k == KT - 1)
                last.then_inc(gates_ps, 1)

                def hidden(e):
                    for f in range(FT):
                        if e:
                            pe.wait_ge(h_ready, (c * NE + e - 1) * FT + f + 1)
                        for k in range(KT):
                            last = nc.tensor.matmul(bank[:, 2 + f, :], w1[:, k, e, f * P:(f + 1) * P], xaT[:, k, :],
                                                    start=k == 0, stop=k == KT - 1)
                        last.then_inc(h_ps, 1)

                pe.wait_ge(weights_ready, c + 1)
                for t in range(TT):
                    last = nc.tensor.transpose(bank[0:NE, 3, t * P:(t + 1) * P], weights[:, t, :], ident[:, :])
                last.then_inc(wT_ps, 1)
                pe.wait_ge(wT_ready, c + 1)
                by_tokens(0, lambda k, t: wT[:, t * P:(t + 1) * P], lambda k: b2[:, :], 1, bias_ps)
                hidden(0)
                for e in range(NE):
                    if e + 1 < NE:
                        hidden(e + 1)
                    pe.wait_ge(h_ready, (c * NE + e + 1) * FT)
                    pe.wait_ge(y_added, c * NE + e + 1)
                    by_tokens(6, lambda k, t: hT[:, e % 2, k, t * P:(t + 1) * P], lambda k: w2[:, e, k, :], FT, y_ps)


def layouts(z):
    p = {k[len("L0_attn_"):]: np.asarray(v) for k, v in z.items() if k.startswith("L0_attn_")}
    f = {k[len("L0_ffn_"):]: np.asarray(v) for k, v in z.items() if k.startswith("L0_ffn_")}

    def columns(v):
        return v.reshape(-1, P).T

    return {
        "x": p["x"].reshape(T, D),
        "in_w": p["in_proj_w"].T, "xp_w": p["x_proj_w"].T, "dt_w": p["dt_proj_w"].T, "out_w": p["out_proj_w"].T,
        "conv_w": p["conv_w"], "conv_b": columns(p["conv_b"]), "dt_b": columns(p["dt_proj_b"]),
        "log_A": p["log_A"], "Dp": columns(p["Dp"]),
        "norm_g": columns(p["norm_g"]), "norm_b": columns(p["norm_b"]), "bq": columns(f["bq"]), "bk": columns(f["bk"]),
        "b1": f["b1"].reshape(NE * FT, P).T,
        **{k: f[k] for k in ("Wq", "Wk", "Wv", "bv", "Wo", "bo", "gW", "gb", "W1", "W2", "b2",
                             "ln1_g", "ln1_b", "ln2_g", "ln2_b")},
    }


def program(nc, a, out):
    scr = Scratch(nc)
    mamba_stage(nc, a, scr)
    attention_stage(nc, a, scr)
    expert_stage(nc, a, scr, out)


def kernel(**inputs):
    import concourse.bacc as bacc
    from concourse.bass_utils import run_bass_kernel_spmd

    nc = bacc.Bacc("TRN2", target_bir_lowering=False, num_devices=1)
    arrays, args = {}, {}
    for name, value in layouts(inputs).items():
        value = np.ascontiguousarray(value)
        arrays[f"in_{name}"] = value
        args[name] = nc.dram_tensor(f"in_{name}", value.shape, mybir.dt.from_np(value.dtype), kind="ExternalInput").ap()
    out = nc.dram_tensor("out", (T, D), F32, kind="ExternalOutput").ap()
    program(nc, args, out)
    result = run_bass_kernel_spmd(nc, [arrays], core_ids=[0]).results[0]["out"]
    return result.reshape(1, T, D)
```

```python
from contextlib import ExitStack

import numpy as np

import concourse.bass as bass
from concourse import mybir

F32 = mybir.dt.float32
BF16 = mybir.dt.bfloat16
ALU = mybir.AluOpType
ACT = mybir.ActivationFunctionType
X = mybir.AxisListType.X

P = 128
T = 4096
D = 256
KT = D // P
CH = 512
NCH = T // CH
TT = CH // P
DI = 512
CT = DI // P
NS = 16
R = 16
TAPS = 4
XP = R + 2 * NS
H = 16
HD = D // H
NE = 8
FF = 512
FT = FF // P
EPS = 1e-5
TERMS = 6
KR = TERMS * HD
SPLITS = 3
VW = 32
NB = H * NCH
NT = T // P
UNITS = NT // 2


def uses_before(b, n, count):
    if n >= RING:
        return b * count + n - RING + 1
    return (b - 1) * count + max(m for m in range(count) if m % RING == n) + 1


class Scratch:

    def __init__(self, nc):
        self.x1 = nc.dram_tensor("x1_scratch", (T, D), F32).ap()
        self.src = nc.dram_tensor("src_scratch", (T, D), F32).ap()
        self.v = nc.dram_tensor("v_scratch", (T, D), F32).ap()
        self.q = nc.dram_tensor("q_scratch", (SPLITS, D, T), BF16).ap()
        self.k = nc.dram_tensor("k_scratch", (SPLITS, D, T), BF16).ap()
        self.attn = nc.dram_tensor("attn_scratch", (T, D), F32).ap()


def settled(engine, sem, value):
    engine.wait_ge(sem, value)


def inverse_deviations(nc, pool, sems, n, mv, powers, met):
    _, var_ready, rstd_ready, rstd, eps_added = sems
    settled(pool, *met)
    pool.wait_ge(var_ready, n)
    nc.gpsimd.tensor_tensor(rstd[:, :], mv[:, :, 1], powers[:, 0, :], ALU.add).then_inc(eps_added, 1)
    settled(pool, *met)
    pool.wait_ge(eps_added, n)
    nc.gpsimd.tensor_tensor(rstd[:, :], rstd[:, :], powers[:, 1, :], ALU.pow).then_inc(rstd_ready, 1)


def layernorm(nc, dve, src, dst, stats, mv, sems, n, done, value):
    stats_done, var_ready, rstd_ready, rstd, _ = sems
    for t in range(TT):
        last = nc.vector.bn_stats(stats[:, t, :], src(t))
    last.then_inc(stats_done, 1)
    dve.wait_ge(stats_done, n)
    nc.vector.memset(rstd[:, 0:1], 0.0)
    for t in range(TT):
        last = nc.vector.bn_aggr(mv[:, t, :], stats[:, t, :])
    last.then_inc(var_ready, 1)
    dve.wait_ge(rstd_ready, n)
    for t in range(TT):
        last = nc.vector.tensor_scalar(dst(t), src(t), mv[:, t, 0:1], rstd[:, t:t + 1], ALU.subtract, ALU.mult)
    last.then_inc(done, 1)
    dve.wait_ge(done, value)


def token_rows(dram, chunk):
    rows = dram[chunk * CH:(chunk + 1) * CH, :] if type(chunk) is int else dram[bass.ds(chunk * CH, CH), :]
    return rows.rearrange("(t p) d -> p t d", p=P)


def mamba_stage(nc, a, scr):
    ctx, stage = ExitStack(), "mamba"
    with ctx:
        def sb(name, shape, dt=F32):
            return ctx.enter_context(nc.sbuf_tensor(f"{stage}_{name}", shape, dt))

        def sem(name):
            return ctx.enter_context(nc.semaphore(f"{stage}_{name}"))

        ident = sb("ident", [P, P])
        w_in = sb("w_in", [P, KT, 2 * DI])
        w_xp = sb("w_xp", [P, CT, XP])
        w_dt = sb("w_dt", [R, DI])
        w_out = sb("w_out", [P, CT, D])
        w_qkv = sb("w_qkv", [P, KT, 3, D])
        conv_w = sb("conv_w", [P, CT, TAPS])
        conv_b = sb("conv_b", [P, CT])
        dt_b = sb("dt_b", [P, CT])
        d_skip = sb("d_skip", [P, CT])
        a_neg = sb("a_neg", [P, CT, NS])
        norm_g = sb("norm_g", [P, KT])
        norm_b = sb("norm_b", [P, KT])
        qk_b = sb("qk_b", [P, 4])
        bv_rows = sb("bv_rows", [P, D])
        conv_diag = sb("conv_diag", [P, CT, TAPS, P])
        skip_diag = sb("skip_diag", [P, CT, P])
        select = sb("select", [P, 2 * NS, P], BF16)
        xin = sb("xin", [P, 2, TT, D])
        xn0 = sb("xn0", [P, 2, TT, D])
        xm = sb("xm", [P, TT, D])
        mo = sb("mo", [P, TT, D])
        srcT = sb("srcT", [P, KT, CH])
        xs = sb("xs", [P, CT, TAPS - 1 + CH])
        zs = sb("zs", [P, CT, CH])
        xc = sb("xc", [P, CT, CH])
        xp = sb("xp", [XP, CH])
        xp_parts = sb("xp_parts", [P, SPLITS, CH], BF16)
        soft = sb("soft", [P, CT, CH])
        delta = sb("delta", [P, CT, CH])
        dx = sb("dx", [P, CT, CH])
        dA = sb("dA", [P, 2, CT, CH])
        dBx = sb("dBx", [P, CT, CH])
        hs = sb("hs", [P, 2, CT, CH])
        c_rows = sb("c_rows", [P, 2, CH])
        hc = sb("hc", [P, 2, CT, CH])
        carry = sb("carry", [P, NS, CT])
        x1c = sb("x1c", [P, TT, D])
        srcc = sb("srcc", [P, TT, D])
        vc = sb("vc", [P, TT, D])
        qk_parts = sb("qk_parts", [P, SPLITS, 4, CH], BF16)
        yg = soft
        qk = dBx
        xmT = hc[:, 0, 0:KT, :]
        stats = sb("stats", [P, TT, 6])
        mv = sb("mv", [P, TT, 2])
        rstd = sb("rstd", [P, TT])
        powers = sb("powers", [P, 2, TT])
        table_warm = sb("table_warm", [P, 1])
        bank = ctx.enter_context(nc.psum_tensor("m_bank", [P, 8, CH], F32))

        (weights_in, x_in, consts_zero, consts_set, signs, diags, xm_ready, xmT_ps, xmT_ready, inproj_ps, halo_done,
         xs_ready, zs_ready, conv_ps, xc_ready, xp_ps, xp_ready, parts_ready, dt_ps, abs_done, relu_done, exp_done,
         soft_ready, delta_ready, dx_ready, bc_ps, dBx_begun, dA_ready, c_ready, dBx_ready, scan_done, carry_done,
         hc_ready, y_added, yg_ready, mo_ps, src_ready, srcT_ps, srcT_ready, qk_ps, qk_biased, qk_hi,
         qk_rest, qk_mid, qk_parts_ready, v_ps, v_ready, stored, xn0_ready, mo_ready,
         mo_normal, x1_ready, stats_done, var_ready, rstd_ready, eps_added) = [sem(n) for n in (
             "weights_in x_in consts_zero consts_set signs diags xm_ready xmT_ps xmT_ready inproj_ps halo_done "
             "xs_ready zs_ready conv_ps xc_ready xp_ps xp_ready parts_ready dt_ps abs_done relu_done exp_done "
             "soft_ready delta_ready dx_ready bc_ps dBx_begun dA_ready c_ready dBx_ready scan_done carry_done "
             "hc_ready y_added yg_ready mo_ps src_ready srcT_ps srcT_ready qk_ps qk_biased qk_hi "
             "qk_rest qk_mid qk_parts_ready v_ps v_ready stored xn0_ready mo_ready "
             "mo_normal x1_ready stats_done var_ready rstd_ready eps_added").split()]
        IN_BANKS = 2, 3, 6, 7, 4, 5, 0, 1
        PARTS = slice(0, CT // 2), slice(CT // 2, CT)
        STORES = 3 + 2 * SPLITS * 2
        ln_sems = stats_done, var_ready, rstd_ready, rstd, eps_added
        block = ctx.enter_context(nc.Block())

        loads = [
            (w_in[:, :, :], a["in_w"].rearrange("(k p) n -> p k n", p=P)),
            (w_xp[:, :, :], a["xp_w"].rearrange("(k p) n -> p k n", p=P)),
            (w_dt[:, :], a["dt_w"]),
            (w_out[:, :, :], a["out_w"].rearrange("(k p) n -> p k n", p=P)),
            (w_qkv[:, :, 0, :], a["Wq"].rearrange("(k p) n -> p k n", p=P)),
            (w_qkv[:, :, 1, :], a["Wk"].rearrange("(k p) n -> p k n", p=P)),
            (w_qkv[:, :, 2, :], a["Wv"].rearrange("(k p) n -> p k n", p=P)),
            (conv_w[:, :, :], a["conv_w"].rearrange("(c p) k -> p c k", p=P)),
            (a_neg[:, :, :], a["log_A"].rearrange("(c p) s -> p c s", p=P)),
            (conv_b[:, :], a["conv_b"]),
            (dt_b[:, :], a["dt_b"]),
            (d_skip[:, :], a["Dp"]),
            (norm_g[:, :], a["norm_g"]),
            (norm_b[:, :], a["norm_b"]),
            (qk_b[:, 0:2], a["bq"]),
            (qk_b[:, 2:4], a["bk"]),
            (bv_rows[:, :], a["bv"].rearrange("(o d) -> o d", o=1).broadcast_to((P, D))),
        ]

        met = weights_in, 16 * len(loads)

        @block.sync
        def _(sp):
            sp.dma_start(xin[:, 0, :, :], token_rows(a["x"], 0)).then_inc(x_in, 16)
            for dst, src in loads:
                sp.dma_start(dst, src).then_inc(weights_in, 16)
            sp.wait_ge(x_in, 16)
            sp.dma_start(xin[:, 1, :, :], token_rows(a["x"], 1)).then_inc(x_in, 16)
            with sp.Fori(0, NCH) as c:
                settled(sp, *met)
                sp.wait_ge(src_ready, c + 1)
                settled(sp, *met)
                sp.wait_ge(x_in, 16 * (c + 2))
                sp.dma_start(xin[:, bass.ds(c % 2, 1), :, :].rearrange("p o t d -> p (o t) d"),
                             token_rows(a["x"], (c + 2) % NCH)).then_inc(x_in, 16)
                sp.dma_start(token_rows(scr.x1, c), x1c[:, :, :]).then_inc(stored, 16)
                sp.dma_start(token_rows(scr.src, c), srcc[:, :, :]).then_inc(stored, 16)
                settled(sp, *met)
                sp.wait_ge(v_ready, c + 2)
                sp.dma_start(token_rows(scr.v, c), vc[:, :, :]).then_inc(stored, 16)
                settled(sp, *met)
                sp.wait_ge(qk_parts_ready, c + 1)
                for n in range(SPLITS):
                    for i, dram in ((0, scr.q), (1, scr.k)):
                        for j in range(2):
                            sp.dma_start(dram[n, j * P:(j + 1) * P, bass.ds(c * CH, CH)],
                                         qk_parts[:, n, 2 * i + j, :]).then_inc(stored, 16)
            sp.wait_ge(x_in, 16 * (NCH + 2))
            sp.wait_ge(stored, 16 * (STORES * NCH + 1))

        @block.gpsimd
        def _(pool):
            nc.gpsimd.memset(ident[:, :], 0.0).then_inc(consts_zero, 1)
            nc.gpsimd.memset(select[:, :, :], 0.0).then_inc(consts_zero, 1)
            nc.gpsimd.memset(xp_parts[:, :, :], 0.0).then_inc(consts_zero, 1)
            pool.wait_ge(consts_zero, 3)
            nc.gpsimd.affine_select(out=ident[:, :], in_=ident[:, :], compare_op=ALU.not_equal, fill=1.0,
                                    base=0, pattern=[[-1, P]], channel_multiplier=1).then_inc(consts_set, 1)
            nc.gpsimd.affine_select(out=select[:, :, :], in_=select[:, :, :], compare_op=ALU.not_equal, fill=1.0,
                                    base=-R, pattern=[[-1, 2 * NS], [0, P]], channel_multiplier=1).then_inc(consts_set, 1)
            nc.gpsimd.memset(carry[:, :, :], 0.0).then_inc(consts_set, 1)
            nc.gpsimd.memset(powers[:, 0, :], EPS).then_inc(consts_set, 1)
            nc.gpsimd.memset(powers[:, 1, :], -0.5).then_inc(consts_set, 1)
            pool.wait_ge(consts_set, 5)
            pool.sem_inc(hc_ready, 2)
            pool.sem_inc(y_added, 2)
            pool.sem_inc(scan_done, 2 * CT)
            pool.sem_inc(dBx_ready, 1)
            pool.sem_inc(c_ready, 1)
            pool.sem_inc(qk_biased, 4)
            pool.sem_inc(v_ready, 1)
            pool.sem_inc(stored, 16)
            for n in range(2):
                inverse_deviations(nc, pool, ln_sems, n + 1, mv, powers, (consts_set, 5))
            with pool.Fori(0, NCH) as c:
                for n in range(2):
                    inverse_deviations(nc, pool, ln_sems, 4 * c + n + 3, mv, powers, met)
                with pool.Fori(0, NS // 2) as s2:
                    for half in range(2):
                        u = c * NS + s2 * 2 + half
                        pool.wait_ge(c_ready, u + 2)
                        pool.wait_ge(scan_done, (u + 3) * CT)
                        pool.wait_ge(y_added, u + 1)
                        nc.gpsimd.tensor_tensor(hc[:, half, :, :], hs[:, half, :, :],
                                                c_rows[:, half:half + 1, :].broadcast_to((P, CT, CH)),
                                                ALU.mult).then_inc(hc_ready, 1)
                for n in range(2, 4):
                    inverse_deviations(nc, pool, ln_sems, 4 * c + n + 3, mv, powers, met)

        @block.vector
        def _(dve):
            dve.wait_ge(consts_set, 5)
            nc.vector.memset(xs[:, :, :], 0.0).then_inc(diags, 1)
            def normal_inputs(c, half, n):
                src = xin[:, half, :, :].rearrange("p o t d -> p (o t) d")
                dst = xn0[:, half, :, :].rearrange("p o t d -> p (o t) d")
                dve.wait_ge(x_in, 16 * (c + 1))
                nc.vector.memset(rstd[:, 0:1], 0.0)
                layernorm(nc, dve, lambda t: src[:, t, :], lambda t: dst[:, t, :], stats, mv, ln_sems, n, xn0_ready, c + 1)
                nc.vector.memset(rstd[:, 0:1], 0.0)
                layernorm(nc, dve, lambda t: dst[:, t, :], lambda t: xm[:, t, :], stats, mv, ln_sems, n + 1, xm_ready, c + 1)

            normal_inputs(0, slice(0, 1), 1)
            dve.wait_ge(weights_in, 16 * len(loads))
            for ct in range(CT):
                for k in range(TAPS):
                    nc.vector.tensor_scalar(conv_diag[:, ct, k, :], ident[:, :], conv_w[:, ct, k:k + 1], None,
                                            ALU.mult).then_inc(diags, 1)
                nc.vector.tensor_scalar(skip_diag[:, ct, :], ident[:, :], d_skip[:, ct:ct + 1], None,
                                        ALU.mult).then_inc(diags, 1)
            dve.wait_ge(signs, 1)
            nc.vector.tensor_scalar(a_neg[:, :, :], a_neg[:, :, :], -1.0, None, ALU.mult).then_inc(diags, 1)
            dve.wait_ge(diags, CT * (TAPS + 1) + 2)
            with dve.Fori(0, NCH) as c:
                dve.wait_ge(xmT_ps, c + 1)
                normal_inputs(c + 1, bass.ds((c + 1) % 2, 1), 4 * c + 3)
                dve.wait_ge(xp_ps, c + 1)
                nc.vector.tensor_copy(xp[:, :], bank[0:XP, 6, :]).then_inc(xp_ready, 1)
                dve.wait_ge(xp_ready, 4 * c + 1)
                nc.vector.tensor_copy(xp_parts[0:XP, 0, :], xp[:, :]).then_inc(xp_ready, 1)
                dve.wait_ge(xp_ready, 4 * c + 2)
                nc.vector.tensor_tensor(qk[0:XP, 0, :], xp[:, :], xp_parts[0:XP, 0, :], ALU.subtract).then_inc(xp_ready, 1)
                dve.wait_ge(xp_ready, 4 * c + 3)
                nc.vector.tensor_copy(xp_parts[0:XP, 1, :], qk[0:XP, 0, :]).then_inc(xp_ready, 1)
                dve.wait_ge(xp_ready, 4 * c + 4)
                nc.vector.tensor_tensor(xp_parts[0:XP, 2, :], qk[0:XP, 0, :], xp_parts[0:XP, 1, :],
                                        ALU.subtract).then_inc(parts_ready, 1)
                for j in range(CT):
                    dve.wait_ge(abs_done, CT * c + j + 1)
                    nc.vector.tensor_scalar(delta[:, j, :], bank[:, j, :], dt_b[:, j:j + 1], 0.0, ALU.add,
                                            ALU.max).then_inc(relu_done, 1)
                dve.wait_ge(relu_done, CT * (c + 1))
                for n, part in enumerate(PARTS):
                    dve.wait_ge(soft_ready, len(PARTS) * c + n + 1)
                    nc.vector.tensor_tensor(delta[:, part, :], delta[:, part, :], soft[:, part, :], ALU.add).then_inc(delta_ready, 1)
                for n, part in enumerate(PARTS):
                    dve.wait_ge(delta_ready, len(PARTS) * c + n + 1)
                    nc.vector.tensor_tensor(dx[:, part, :], delta[:, part, :], xc[:, part, :], ALU.mult).then_inc(dx_ready, 1)
                dve.wait_ge(dx_ready, len(PARTS) * (c + 1))
                nc.vector.memset(rstd[:, 0:1], 0.0)
                with dve.Fori(0, NS // 2) as s2:
                    for half in range(2):
                        u = c * NS + s2 * 2 + half
                        own_carry = bass.ds(s2 * 2 + half, 1)
                        dve.wait_ge(bc_ps, u + 1)
                        for part, done in zip(PARTS, (dBx_begun, dBx_ready)):
                            nc.vector.tensor_tensor(dBx[:, part, :], dx[:, part, :],
                                                    bank[:, 4 + half:5 + half, :].broadcast_to((P, CT // 2, CH)),
                                                    ALU.mult).then_inc(done, 1)
                        dve.wait_ge(dA_ready, (u + 1) * CT)
                        dve.wait_ge(hc_ready, u + 1)
                        dve.wait_ge(dBx_begun, u + 1)
                        for ct in range(CT):
                            if ct == CT // 2:
                                dve.wait_ge(dBx_ready, u + 2)
                            nc.vector.tensor_tensor_scan(hs[:, half, ct, :], dA[:, half, ct, :], dBx[:, ct, :],
                                                         carry[:, own_carry, ct], ALU.mult, ALU.add).then_inc(scan_done, 1)
                        dve.wait_ge(scan_done, (u + 3) * CT)
                        nc.vector.tensor_scalar(carry[:, own_carry, :].rearrange("p o c -> p (o c)"),
                                                hs[:, half, :, CH - 1], 1.0, None, ALU.mult).then_inc(carry_done, 1)
                dve.wait_ge(carry_done, NS * (c + 1))
                nc.vector.tensor_copy(xs[:, :, 0:TAPS - 1], xs[:, :, CH:CH + TAPS - 1]).then_inc(halo_done, 1)
                dve.wait_ge(halo_done, c + 1)
                dve.wait_ge(y_added, NS * (c + 1) + 2)
                nc.vector.tensor_tensor(yg[:, :, :], bank[:, 0:CT, :], zs[:, :, :], ALU.mult).then_inc(yg_ready, 1)
                dve.wait_ge(mo_ps, c + 1)
                tokens_ps = bank[:, 4:6, :].rearrange("p b (h d) -> p (b h) d", d=D)
                nc.vector.tensor_tensor(mo[:, :, :], tokens_ps, xn0[:, bass.ds(c % 2, 1), :, :].rearrange("p o t d -> p (o t) d"),
                                        ALU.add).then_inc(mo_ready, 1)
                dve.wait_ge(mo_ready, c + 1)
                layernorm(nc, dve, lambda t: mo[:, t, :], lambda t: mo[:, t, :], stats, mv, ln_sems, 4 * c + 5, mo_normal, c + 1)
                dve.wait_ge(stored, 16 * (STORES * c + 1))
                nc.vector.tensor_tensor(x1c[:, :, :], mo[:, :, :], xin[:, bass.ds(c % 2, 1), :, :].rearrange("p o t d -> p (o t) d"),
                                        ALU.add).then_inc(x1_ready, 1)
                dve.wait_ge(x1_ready, c + 1)
                layernorm(nc, dve, lambda t: x1c[:, t, :], lambda t: srcc[:, t, :], stats, mv, ln_sems, 4 * c + 6, src_ready, c + 1)
                dve.wait_ge(qk_hi, c + 1)
                nc.vector.tensor_tensor(qk[:, :, :], qk[:, :, :], qk_parts[:, 0, :, :], ALU.subtract).then_inc(qk_rest, 1)
                dve.wait_ge(v_ps, c + 1)
                nc.vector.tensor_tensor(vc[:, :, :], tokens_ps, bv_rows[:, :].rearrange("p (o d) -> p o d", o=1)
                                        .broadcast_to((P, TT, D)), ALU.add).then_inc(v_ready, 1)
                dve.wait_ge(qk_mid, c + 1)
                nc.vector.tensor_tensor(qk_parts[:, 2, :, :], qk[:, :, :], qk_parts[:, 1, :, :],
                                        ALU.subtract).then_inc(qk_parts_ready, 1)
                dve.wait_ge(qk_parts_ready, c + 1)

        @block.scalar
        def _(act):
            act.wait_ge(weights_in, 16 * len(loads))
            nc.scalar.activation(a_neg[:, :, :], a_neg[:, :, :], ACT.Exp).then_inc(signs, 1)
            act.wait_ge(diags, 1)

            def in_projected(c):
                act.wait_ge(xmT_ps, c + 1)
                for k in range(KT):
                    nc.scalar.activation(xmT[:, k, :], bank[:, k, :], ACT.Identity, bias=norm_b[:, k:k + 1],
                                         scale=norm_g[:, k:k + 1]).then_inc(xmT_ready, 1)
                for j in range(CT):
                    act.wait_ge(inproj_ps, 2 * CT * c + j + 1)
                    nc.scalar.activation(xs[:, j, TAPS - 1:], bank[:, IN_BANKS[j], :], ACT.Copy).then_inc(xs_ready, 1)
                for j in range(CT):
                    act.wait_ge(inproj_ps, 2 * CT * c + CT + j + 1)
                    nc.scalar.activation(zs[:, j, :], bank[:, IN_BANKS[CT + j], :], ACT.Silu).then_inc(zs_ready, 1)

            in_projected(0)
            act.wait_ge(diags, CT * (TAPS + 1) + 2)
            with act.Fori(0, NCH) as c:
                for j in range(CT):
                    act.wait_ge(conv_ps, CT * c + j + 1)
                    nc.scalar.activation(xc[:, j, :], bank[:, j, :], ACT.Silu,
                                         bias=conv_b[:, j:j + 1]).then_inc(xc_ready, 1)
                for j in range(CT):
                    act.wait_ge(dt_ps, CT * c + j + 1)
                    nc.scalar.activation(soft[:, j, :], bank[:, j, :], ACT.Abs, bias=dt_b[:, j:j + 1]).then_inc(abs_done, 1)
                act.wait_ge(abs_done, CT * (c + 1))
                nc.scalar.activation(soft[:, :, :], soft[:, :, :], ACT.Exp, scale=-1.0).then_inc(exp_done, 1)
                act.wait_ge(exp_done, 2 * c + 1)
                for part in PARTS:
                    nc.scalar.activation(soft[:, part, :], soft[:, part, :], ACT.Ln, bias=1.0).then_inc(soft_ready, 1)
                nc.scalar.activation(table_warm[:, :], conv_b[:, 0:1], ACT.Exp, scale=0.0).then_inc(exp_done, 1)
                act.wait_ge(delta_ready, len(PARTS) * (c + 1))
                act.wait_ge(exp_done, 2 * c + 2)
                with act.Fori(0, NS // 2) as s2:
                    for half in range(2):
                        u = c * NS + s2 * 2 + half
                        act.wait_ge(scan_done, (u + 1) * CT)
                        for ct in range(CT):
                            nc.scalar.activation(dA[:, half, ct, :], delta[:, ct, :], ACT.Exp,
                                                 scale=a_neg[:, ct, bass.ds(s2 * 2 + half, 1)]).then_inc(dA_ready, 1)
                        act.wait_ge(bc_ps, u + 1)
                        act.wait_ge(hc_ready, u + 1)
                        nc.scalar.activation(c_rows[:, half, :], bank[:, 6 + half, :], ACT.Copy).then_inc(c_ready, 1)
                in_projected(c + 1)
                act.wait_ge(srcT_ps, c + 1)
                nc.scalar.activation(srcT[:, :, :], bank[:, 0:KT, :], ACT.Copy).then_inc(srcT_ready, 1)
                for i, b in enumerate((2, 3, 6, 7)):
                    act.wait_ge(qk_ps, 4 * c + i + 1)
                    nc.scalar.activation(qk[:, i, :], bank[:, b, :], ACT.Identity, bias=qk_b[:, i:i + 1]
                                         ).then_inc(qk_biased, 1)
                act.wait_ge(qk_biased, 4 * (c + 2))
                nc.scalar.activation(qk_parts[:, 0, :, :], qk[:, :, :], ACT.Copy).then_inc(qk_hi, 1)
                act.wait_ge(qk_rest, c + 1)
                nc.scalar.activation(qk_parts[:, 1, :, :], qk[:, :, :], ACT.Copy).then_inc(qk_mid, 1)

        @block.tensor
        def _(pe):
            pe.wait_ge(consts_set, 5)

            def transposed(src, done):
                for k in range(KT):
                    for t in range(TT):
                        last = nc.tensor.transpose(bank[:, k, t * P:(t + 1) * P], src[:, t, k * P:(k + 1) * P],
                                                   ident[:, :])
                last.then_inc(done, 1)

            def in_projection(c, first=False):
                pe.wait_ge(xm_ready, c + 1)
                transposed(xm, xmT_ps)
                pe.wait_ge(c_ready, NS * c + 1)
                pe.wait_ge(xmT_ready, KT * (c + 1))
                for j in range(2 * CT):
                    if j == CT and not first:
                        pe.wait_ge(mo_ready, c)
                    for k in range(KT):
                        last = nc.tensor.matmul(bank[:, IN_BANKS[j], :], w_in[:, k, j * P:(j + 1) * P], xmT[:, k, :],
                                                start=k == 0, stop=k == KT - 1)
                    last.then_inc(inproj_ps, 1)

            pe.wait_ge(weights_in, 16 * len(loads))
            in_projection(0, True)
            pe.wait_ge(diags, CT * (TAPS + 1) + 2)
            with pe.Fori(0, NCH) as c:
                pe.wait_ge(zs_ready, CT * (c + 1))
                pe.wait_ge(qk_biased, 4 * c + 2)
                for j in range(CT):
                    pe.wait_ge(xs_ready, CT * c + j + 1)
                    for k in range(TAPS):
                        last = nc.tensor.matmul(bank[:, j, :], conv_diag[:, j, k, :], xs[:, j, k:k + CH],
                                                start=k == 0, stop=k == TAPS - 1)
                    last.then_inc(conv_ps, 1)
                pe.wait_ge(qk_biased, 4 * (c + 1))
                pe.wait_ge(v_ready, c + 1)
                for j in range(CT):
                    pe.wait_ge(xc_ready, CT * c + j + 1)
                    last = nc.tensor.matmul(bank[0:XP, 6, :], w_xp[:, j, :], xc[:, j, :], start=j == 0, stop=j == CT - 1)
                last.then_inc(xp_ps, 1)
                pe.wait_ge(xp_ready, 4 * c + 1)
                for j in range(CT):
                    nc.tensor.matmul(bank[:, j, :], w_dt[:, j * P:(j + 1) * P], xp[0:R, :],
                                     start=True, stop=True).then_inc(dt_ps, 1)
                pe.wait_ge(parts_ready, c + 1)

                def state_rows(s, half):
                    for i in range(2):
                        for n in range(SPLITS):
                            last = nc.tensor.matmul(
                                bank[:, 4 + 2 * i + half, :],
                                select[:, bass.ds(i * NS + s, 1), :].rearrange("r o p -> r (o p)"), xp_parts[:, n, :],
                                start=n == 0, stop=n == SPLITS - 1)
                    last.then_inc(bc_ps, 1)

                def add_state(u, half):
                    pe.wait_ge(hc_ready, u + 3)
                    for ct in range(CT):
                        last = nc.tensor.matmul(bank[:, ct, :], ident[:, :], hc[:, half, ct, :],
                                                start=False, stop=True, skip_group_check=True)
                    last.then_inc(y_added, 1)

                for half in range(2):
                    state_rows(half, half)
                pe.wait_ge(relu_done, CT * (c + 1))
                for ct in range(CT):
                    nc.tensor.matmul(bank[:, ct, :], skip_diag[:, ct, :], xc[:, ct, :], start=True, stop=True,
                                     skip_group_check=True)
                with pe.Fori(0, NS // 2 - 1) as s2:
                    for half in range(2):
                        u = c * NS + s2 * 2 + half
                        pe.wait_ge(dBx_ready, u + 2)
                        pe.wait_ge(c_ready, u + 2)
                        state_rows(s2 * 2 + half + 2, half)
                        add_state(u, half)
                for half in range(2):
                    add_state(c * NS + NS - 2 + half, half)
                pe.wait_ge(yg_ready, c + 1)
                for t in range(TT):
                    for ct in range(CT):
                        last = nc.tensor.matmul(bank[:, 4 + t // 2, (t % 2) * D:(t % 2 + 1) * D],
                                                yg[:, ct, t * P:(t + 1) * P], w_out[:, ct, :],
                                                start=ct == 0, stop=ct == CT - 1)
                last.then_inc(mo_ps, 1)
                in_projection(c + 1)
                pe.wait_ge(zs_ready, CT * (c + 2))
                pe.wait_ge(src_ready, c + 1)
                transposed(srcc, srcT_ps)
                pe.wait_ge(srcT_ready, c + 1)
                for i, b in enumerate((2, 3, 6, 7)):
                    for k in range(KT):
                        last = nc.tensor.matmul(bank[:, b, :], w_qkv[:, k, i // 2, (i % 2) * P:(i % 2 + 1) * P],
                                                srcT[:, k, :], start=k == 0, stop=k == KT - 1)
                    last.then_inc(qk_ps, 1)
                for t in range(TT):
                    for k in range(KT):
                        last = nc.tensor.matmul(bank[:, 4 + t // 2, (t % 2) * D:(t % 2 + 1) * D],
                                                srcT[:, k, t * P:(t + 1) * P], w_qkv[:, k, 2, :],
                                                start=k == 0, stop=k == KT - 1)
                last.then_inc(v_ps, 1)


MAX_JOBS = TT * NCH
EARLY = 16
PAIRS = UNITS // 2
RING = 3
SUMS_AT = 2
ROWS_AT = 1
ROWS_JOB = EARLY - 4 - (3 - ROWS_AT)
NP = 4


def attention_stage(nc, a, scr):
    ctx, stage = ExitStack(), "attention"
    with ctx:
        def sb(name, shape, dt=F32):
            return ctx.enter_context(nc.sbuf_tensor(f"{stage}_{name}", shape, dt))

        def sem(name):
            return ctx.enter_context(nc.semaphore(f"{stage}_{name}"))

        qst = sb("qst", [P, 2 * T], BF16)
        kst = sb("kst", [P, 2 * T], BF16)
        vtok = sb("vtok", [P, NT, D])
        vh = sb("vh", [P, NT, VW])
        probs = sb("probs", [P, NP, 2, CH])
        oT = sb("oT", [P, CH])
        attn = sb("attn", [P, NT, D])
        identb = sb("identb", [P, P], BF16)
        gather = sb("gather", [P, HD + 1])
        mx = sb("mx", [P, MAX_JOBS])
        mx_early = sb("mx_early", [P, EARLY])
        neg_max = sb("neg_max", [P, TT])
        max_parts = sb("max_parts", [P, TT, SPLITS], BF16)
        sums = sb("sums", [P, TT])
        table_warm = sb("table_warm", [P, 1])
        bank = ctx.enter_context(nc.psum_tensor(f"{stage}_bank", [P, 8, CH], F32))
        SCORES, MAXES, OUT, SMALL = 0, 3, 6, 7

        (zeroed, consts, q_in, v_in, heads_in, vh_ready, scored, exp_done, pv_done, max_scored, max_done, negated,
         parts_done, max_rows, rows_ready, oT_ready, summed, inverted, normal, early_moved, stored) = [sem(n) for n in (
             "zeroed consts q_in v_in heads_in vh_ready scored exp_done pv_done max_scored max_done negated "
             "parts_done max_rows rows_ready oT_ready summed inverted normal early_moved stored").split()]
        HEAD_LOADS = 2 * TERMS
        block = ctx.enter_context(nc.Block())

        def ring(b):
            return (b % (2 * NCH)) * CH

        def load_head(sp, h, half):
            rows = bass.ds(h * HD, HD)
            cols = slice(half * T, (half + 1) * T) if type(half) is int else bass.ds(half * T, T)
            for i, n in enumerate((0, 0, 0, 1, 1, 2)):
                sp.dma_start(qst[i * HD:(i + 1) * HD, cols], scr.q[n, rows, :]).then_inc(heads_in, 16)
            for i, n in ((0, 3), (3, 2), (5, 1)):
                for j in range(n):
                    sp.dma_start(kst[(i + j) * HD:(i + j + 1) * HD, cols], scr.k[j, rows, :]).then_inc(heads_in, 16)

        @block.sync
        def _(sp):
            sp.wait_ge(consts, 1)
            load_head(sp, 0, 0)
            sp.dma_start(vtok[:, :, :], scr.v.rearrange("(t p) d -> p t d", p=P)).then_inc(v_in, 16)
            sp.wait_ge(heads_in, 16 * HEAD_LOADS)
            load_head(sp, 1, 1)
            with sp.Fori(2, H) as h:
                sp.wait_ge(heads_in, 16 * HEAD_LOADS * h)
                settled(sp, consts, 1)
                sp.wait_ge(pv_done, NCH * (h - 1) * PAIRS)
                load_head(sp, h, h % 2)
            sp.wait_ge(heads_in, 16 * HEAD_LOADS * H)
            sp.wait_ge(normal, NB)
            sp.dma_start(scr.attn.rearrange("(t p) d -> p t d", p=P), attn[:, :, :]).then_inc(stored, 16)
            sp.wait_ge(stored, 16)

        @block.gpsimd
        def _(pool):
            nc.gpsimd.memset(kst[96:128, :], 1.0).then_inc(consts, 1)
            pool.wait_ge(consts, 1)
            nc.gpsimd.memset(identb[:, :], 0.0).then_inc(zeroed, 1)
            nc.gpsimd.memset(gather[:, :], 0.0).then_inc(zeroed, 1)
            nc.gpsimd.memset(vh[:, :, :], 0.0).then_inc(zeroed, 1)
            pool.wait_ge(zeroed, 3)
            nc.gpsimd.memset(vh[:, :, HD:HD + 1], 1.0).then_inc(consts, 1)
            nc.gpsimd.affine_select(out=identb[:, :], in_=identb[:, :], compare_op=ALU.not_equal, fill=1.0,
                                    base=0, pattern=[[-1, P]], channel_multiplier=1).then_inc(consts, 1)
            for j in range(P // VW):
                nc.gpsimd.affine_select(out=gather[:, :], in_=gather[:, :], compare_op=ALU.not_equal, fill=1.0,
                                        base=-VW * j, pattern=[[-1, HD + 1]], channel_multiplier=1).then_inc(consts, 1)
                pool.wait_ge(consts, 4 + j)
            pool.wait_ge(v_in, 16)
            pool.sem_inc(summed, 1)
            nc.gpsimd.tensor_copy(vh[:, :, 0:HD], vtok[:, :, 0:HD]).then_inc(vh_ready, 1)
            with pool.Fori(1, H) as h:
                pool.wait_ge(pv_done, NCH * h * PAIRS)
                settled(pool, v_in, 16)
                nc.gpsimd.tensor_copy(vh[:, :, 0:HD], vtok[:, :, bass.ds(h * HD, HD)]).then_inc(vh_ready, 1)

        CONSTS = 3 + P // VW

        @block.scalar
        def _(act):
            act.wait_ge(consts, CONSTS)
            nc.scalar.activation(table_warm[:, :], gather[:, 0:1], ACT.Exp).then_inc(zeroed, 1)

            def take_sums(b):
                act.wait_ge(pv_done, (b + 1) * PAIRS)
                act.wait_ge(summed, b + 1)
                nc.scalar.activation(oT[:, :], bank[:, OUT, :], ACT.Copy).then_inc(oT_ready, 1)

            def exponentials(b, first):
                for n in range(NT):
                    act.wait_ge(scored, b * NT + n + 1)
                    if n % 2 == 0 and not (first and n < 2 * NP):
                        act.wait_ge(pv_done, b * PAIRS + n // 4 - 1)
                    nc.scalar.activation(probs[:, n // 2 % NP, n % 2, :], bank[:, SCORES + n % RING, :],
                                         ACT.Exp, scale=float(HD) ** -0.5).then_inc(exp_done, 1)
                    if n == SUMS_AT and not first:
                        take_sums(b - 1)

            exponentials(0, True)
            with act.Fori(1, NB) as b:
                exponentials(b, False)
            take_sums(NB - 1)

        @block.vector
        def _(dve):
            dve.wait_ge(consts, CONSTS)

            small = bank[:, SMALL, 0:TT * VW].rearrange("p (t w) -> p t w", w=VW)

            def scale_by_sums(b):
                dve.wait_ge(inverted, b + 1)
                tiles = slice(b % NCH * TT, b % NCH * TT + TT) if type(b) is int else bass.ds(b % NCH * TT, TT)
                head = slice(b // NCH * HD, b // NCH * HD + HD) if type(b) is int else bass.ds(b // NCH * HD, HD)
                nc.vector.tensor_tensor(attn[:, tiles, head], small[:, :, 0:HD],
                                        sums[:, :].rearrange("p (t o) -> p t o", o=1).broadcast_to((P, TT, HD)),
                                        ALU.mult).then_inc(normal, 1)

            def normalise(b):
                dve.wait_ge(summed, b + 2)
                nc.vector.reciprocal(sums[:, :], small[:, :, HD]).then_inc(inverted, 1)
                scale_by_sums(b)

            def take_maxima(b, n0, n1):
                for n in range(n0, n1):
                    dve.wait_ge(max_scored, b * MAX_JOBS + n + 1)
                    dst = mx_early if n < EARLY else mx
                    nc.vector.reduce_max(dst[:, n:n + 1], bank[:, MAXES + n % RING, :], X).then_inc(max_done, 1)

            def maxima(b, normal_of, early):
                dve.wait_ge(max_done, b * MAX_JOBS + EARLY)
                nc.vector.tensor_copy(mx[:, 0:EARLY], mx_early[:, :]).then_inc(early_moved, 1)
                take_maxima(b, EARLY, EARLY + 4)
                if normal_of is not None:
                    dve.wait_ge(summed, normal_of + 2)
                    nc.vector.reciprocal(sums[:, :], small[:, :, HD]).then_inc(inverted, 1)
                    take_maxima(b, EARLY + 4, EARLY + 5)
                    scale_by_sums(normal_of)
                    take_maxima(b, EARLY + 5, MAX_JOBS)
                else:
                    take_maxima(b, EARLY + 4, MAX_JOBS)

                def early_job(k):
                    if early:
                        take_maxima(b + 1, k, k + 1)

                dve.wait_ge(max_done, b * MAX_JOBS + MAX_JOBS)
                nc.vector.tensor_reduce(neg_max[:, :], mx[:, :].rearrange("p (t c) -> p t c", c=NCH), X, ALU.max, negate=True).then_inc(negated, 1)
                early_job(0)
                dve.wait_ge(negated, b + 1)
                nc.vector.tensor_copy(max_parts[:, :, 0], neg_max[:, :]).then_inc(parts_done, 1)
                early_job(1)
                dve.wait_ge(parts_done, 5 * b + 1)
                nc.vector.tensor_tensor(neg_max[:, :], neg_max[:, :], max_parts[:, :, 0], ALU.subtract).then_inc(parts_done, 1)
                early_job(2)
                dve.wait_ge(parts_done, 5 * b + 2)
                nc.vector.tensor_copy(max_parts[:, :, 1], neg_max[:, :]).then_inc(parts_done, 1)
                early_job(3)
                dve.wait_ge(parts_done, 5 * b + 3)
                nc.vector.tensor_tensor(neg_max[:, :], neg_max[:, :], max_parts[:, :, 1], ALU.subtract).then_inc(parts_done, 1)
                early_job(4)
                dve.wait_ge(parts_done, 5 * b + 4)
                nc.vector.tensor_copy(max_parts[:, :, 2], neg_max[:, :]).then_inc(parts_done, 1)
                for k in range(5, ROWS_JOB):
                    early_job(k)
                dve.wait_ge(max_rows, b + 1)
                cols = slice(ring(b), ring(b) + CH) if type(b) is int else bass.ds(ring(b), CH)
                nc.vector.tensor_copy(qst[KR:KR + SPLITS, cols], bank[KR:KR + SPLITS, SMALL, :]).then_inc(rows_ready, 1)
                for k in range(ROWS_JOB, EARLY):
                    early_job(k)

            take_maxima(0, 0, EARLY)
            maxima(0, None, True)
            maxima(1, None, True)
            with dve.Fori(2, NB - 1) as b:
                maxima(b, b - 2, True)
            maxima(NB - 1, NB - 3, False)
            normalise(NB - 2)
            normalise(NB - 1)

        @block.tensor
        def _(pe):
            pe.wait_ge(consts, CONSTS)

            def columns(start, n):
                return slice(start, start + n) if type(start) is int else bass.ds(start, n)

            def score_product(b, n, first=False):
                if not (first and n < RING):
                    pe.wait_ge(exp_done, uses_before(b, n, NT))
                nc.tensor.matmul(bank[:, SCORES + n % RING, :],
                                 kst[0:KR + SPLITS, columns(b // NCH % 2 * T + n * P, P)],
                                 qst[0:KR + SPLITS, columns(ring(b), CH)], start=True, stop=True).then_inc(scored, 1)

            def max_job(b, n, first=False):
                if not (first and n < RING):
                    pe.wait_ge(max_done, uses_before(b, n, MAX_JOBS))
                nc.tensor.matmul(bank[:, MAXES + n % RING, :],
                                 qst[0:KR, columns(ring(b) + n // NCH * P, P)],
                                 kst[0:KR, columns(b // NCH % 2 * T + n % NCH * CH, CH)],
                                 start=True, stop=True).then_inc(max_scored, 1)

            def max_to_rows(b):
                pe.wait_ge(parts_done, 5 * (b + 1))
                for t in range(TT):
                    last = nc.tensor.matmul(bank[KR:KR + SPLITS, SMALL, t * P:(t + 1) * P], max_parts[:, t, :],
                                            identb[:, :], start=True, stop=True)
                last.then_inc(max_rows, 1)

            def value_pair(b, v):
                pe.wait_ge(exp_done, b * NT + 4 * v + 4)
                for g in range(4):
                    last = nc.tensor.matmul(bank[VW * g:VW * (g + 1), OUT, :], vh[:, 4 * v + g, :],
                                            probs[:, (2 * v + g // 2) % NP, g % 2, :], start=v == 0, stop=v == PAIRS - 1)
                last.then_inc(pv_done, 1)

            def add_groups(b):
                pe.wait_ge(oT_ready, b + 1)
                for t in range(TT):
                    last = nc.tensor.matmul(bank[:, SMALL, t * VW:t * VW + HD + 1], oT[:, t * P:(t + 1) * P],
                                            gather[:, :], start=True, stop=True)
                last.then_inc(summed, 1)

            def one_block(b, first, left):
                jobs = [(b + 1, n) for n in range(EARLY, MAX_JOBS)] * (left > 0) + [(b + 2, n) for n in range(EARLY)] * (left > 1)

                def next_job():
                    if jobs:
                        max_job(*jobs.pop(0))

                if left > 1:
                    pe.wait_ge(heads_in, ((b + 2) // NCH + 1) * 16 * HEAD_LOADS)
                for v in range(PAIRS):
                    for n in range(4 * v + RING, 4 * v + RING + 4):
                        if n < NT:
                            score_product(b, n)
                        elif left:
                            if n == NT:
                                pe.wait_ge(rows_ready, b + 2)
                            score_product(b + 1, n - NT)
                        next_job()
                        if v == PAIRS - 2 and n == 4 * v + RING + ROWS_AT and left:
                            if not first:
                                pe.wait_ge(normal, b)
                            max_to_rows(b + 1)
                    if v == 0:
                        pe.wait_ge(vh_ready, b // NCH + 1)
                        if not first:
                            pe.wait_ge(oT_ready, b)
                    value_pair(b, v)
                    if v == 0 and not first:
                        add_groups(b - 1)

            pe.wait_ge(heads_in, 16 * HEAD_LOADS)
            for n in range(MAX_JOBS):
                max_job(0, n, True)
            for n in range(ROWS_JOB):
                max_job(1, n)
            max_to_rows(0)
            for n in range(ROWS_JOB, EARLY):
                max_job(1, n)
            pe.wait_ge(rows_ready, 1)
            for n in range(RING):
                score_product(0, n, True)
            one_block(0, True, 2)
            with pe.Fori(1, NB - 2) as b:
                one_block(b, False, 2)
            one_block(NB - 2, False, 1)
            one_block(NB - 1, False, 0)
            pe.wait_ge(normal, NB - 1)
            add_groups(NB - 1)


NEXT_AT = 2


def expert_stage(nc, a, scr, out):
    ctx, stage = ExitStack(), "experts"
    with ctx:
        def sb(name, shape, dt=F32):
            return ctx.enter_context(nc.sbuf_tensor(f"{stage}_{name}", shape, dt))

        def sem(name):
            return ctx.enter_context(nc.semaphore(f"{stage}_{name}"))

        w1 = sb("w1", [P, KT, NE, FF])
        w2 = sb("w2", [P, NE, FT, D])
        wo = sb("wo", [P, KT, D])
        gw = sb("gw", [P, KT, NE])
        b1 = sb("b1", [P, NE * FT])
        b2 = sb("b2", [NE, D])
        rows = {n: sb(n + "_rows", [P, D]) for n in ("bo", "ln1_g", "ln1_b", "ln2_g", "ln2_b")}
        gb_rows = sb("gb_rows", [P, NE])
        ident = sb("ident", [P, P])
        before = sb("before", [P, NE, NE])
        powers = sb("powers", [P, 2, TT])
        table_warm = sb("table_warm", [P, 1])
        at_in = sb("at_in", [P, TT, D])
        src_in = sb("src_in", [P, TT, D])
        x1_in = sb("x1_in", [P, TT, D])
        atT = sb("atT", [P, KT, CH])
        xa = sb("xa", [P, TT, D])
        xn = sb("xn", [P, TT, D])
        xaT = sb("xaT", [P, KT, CH])
        hT = sb("hT", [P, 2, FT, CH])
        acc = sb("acc", [P, TT, D])
        outc = sb("outc", [P, TT, D])
        logits = sb("logits", [P, TT, NE])
        gates = sb("gates", [P, TT, NE])
        top = sb("top", [P, TT])
        over = sb("over", [P, TT, NE, NE])
        ties = sb("ties", [P, TT, NE, NE])
        rank = sb("rank", [P, TT, NE])
        weights = sb("weights", [P, TT, NE])
        wT = sb("wT", [NE, CH])
        stats = sb("stats", [P, TT, 6])
        mv = sb("mv", [P, TT, 2])
        rstd = sb("rstd", [P, TT])
        bank = ctx.enter_context(nc.psum_tensor(f"{stage}_bank", [P, 8, CH], F32))

        (rows_in, weights_in, at_loaded, src_loaded, x1_loaded, zeroed, consts, atT_ps, atT_ready, wo_ps, added, src_used,
         normal1, xa_ready, xaT_ps, xaT_ready, gates_ps, gate_steps, shifted, exp_done, weights_ready, wT_ps, wT_ready,
         bias_ps, h_ps, h_ready, y_ps, y_added, normal2, out_ready, stored, stats_done, var_ready,
         rstd_ready, eps_added, moe_normal, attn_added, scaled) = [sem(n) for n in (
             "rows_in weights_in at_loaded src_loaded x1_loaded zeroed consts atT_ps atT_ready wo_ps added src_used "
             "normal1 xa_ready xaT_ps xaT_ready gates_ps gate_steps shifted exp_done weights_ready wT_ps wT_ready "
             "bias_ps h_ps h_ready y_ps y_added normal2 out_ready stored stats_done var_ready "
             "rstd_ready eps_added moe_normal attn_added scaled").split()]
        ln_sems = stats_done, var_ready, rstd_ready, rstd, eps_added
        block = ctx.enter_context(nc.Block())

        def to_rows(name, width):
            return a[name].rearrange("(o d) -> o d", o=1).broadcast_to((P, width))

        loads = [
            (wo[:, :, :], a["Wo"].rearrange("(k p) n -> p k n", p=P)),
            (gw[:, :, :], a["gW"].rearrange("(k p) n -> p k n", p=P)),
            (b1[:, :], a["b1"]),
            (b2[:, :], a["b2"]),
            (gb_rows[:, :], to_rows("gb", NE)),
            *[(r[:, :], to_rows(n, D)) for n, r in rows.items()],
        ]
        expert_loads = [
            *[(w1[:, k, :, :], a["W1"][:, k * P:(k + 1) * P, :].rearrange("e p f -> p e f")) for k in range(KT)],
            *[(w2[:, e, :, :], a["W2"][e, :, :].rearrange("(f p) d -> p f d", p=P)) for e in range(NE)],
        ]
        met = rows_in, 16 * len(loads)

        @block.sync
        def _(sp):
            sp.dma_start(at_in[:, :, :], token_rows(scr.attn, 0)).then_inc(at_loaded, 16)
            sp.dma_start(src_in[:, :, :], token_rows(scr.src, 0)).then_inc(src_loaded, 16)
            sp.dma_start(x1_in[:, :, :], token_rows(scr.x1, 0)).then_inc(x1_loaded, 16)
            for dst, src in loads:
                sp.dma_start(dst, src).then_inc(rows_in, 16)
            for dst, src in expert_loads:
                sp.dma_start(dst, src).then_inc(weights_in, 16)
            sp.wait_ge(*met)
            sp.wait_ge(atT_ps, 1)
            sp.dma_start(at_in[:, :, :], token_rows(scr.attn, 1)).then_inc(at_loaded, 16)
            sp.wait_ge(src_used, 1)
            sp.dma_start(src_in[:, :, :], token_rows(scr.src, 1)).then_inc(src_loaded, 16)
            with sp.Fori(0, NCH) as c:
                settled(sp, *met)
                sp.wait_ge(atT_ps, c + 2)
                sp.dma_start(at_in[:, :, :], token_rows(scr.attn, (c + 2) % NCH)).then_inc(at_loaded, 16)
                settled(sp, *met)
                sp.wait_ge(src_used, c + 2)
                sp.dma_start(src_in[:, :, :], token_rows(scr.src, (c + 2) % NCH)).then_inc(src_loaded, 16)
                settled(sp, *met)
                sp.wait_ge(out_ready, c + 1)
                sp.dma_start(x1_in[:, :, :], token_rows(scr.x1, (c + 1) % NCH)).then_inc(x1_loaded, 16)
                sp.dma_start(token_rows(out, c), outc[:, :, :]).then_inc(stored, 16)
            sp.wait_ge(at_loaded, 16 * (NCH + 2))
            sp.wait_ge(src_loaded, 16 * (NCH + 2))
            sp.wait_ge(x1_loaded, 16 * (NCH + 1))
            sp.wait_ge(stored, 16 * (NCH + 1))

        @block.gpsimd
        def _(pool):
            nc.gpsimd.memset(ident[:, :], 0.0).then_inc(zeroed, 1)
            nc.gpsimd.memset(before[:, :, :], 1.0).then_inc(zeroed, 1)
            nc.gpsimd.memset(powers[:, 0, :], EPS).then_inc(zeroed, 1)
            nc.gpsimd.memset(powers[:, 1, :], -0.5).then_inc(zeroed, 1)
            pool.wait_ge(zeroed, 4)
            nc.gpsimd.affine_select(out=ident[:, :], in_=ident[:, :], compare_op=ALU.not_equal, fill=1.0,
                                    base=0, pattern=[[-1, P]], channel_multiplier=1).then_inc(consts, 1)
            nc.gpsimd.affine_select(out=before[:, :, :], in_=before[:, :, :], compare_op=ALU.is_gt, fill=0.0,
                                    base=0, pattern=[[1, NE], [-1, NE]], channel_multiplier=0).then_inc(consts, 1)
            pool.wait_ge(*met)
            pool.sem_inc(y_added, 1)
            pool.sem_inc(stored, 16)
            inverse_deviations(nc, pool, ln_sems, 1, mv, powers, met)
            with pool.Fori(0, NCH) as c:
                for n in range(3):
                    inverse_deviations(nc, pool, ln_sems, 3 * c + n + 2, mv, powers, met)

        @block.scalar
        def _(act):
            act.wait_ge(consts, 2)
            act.wait_ge(*met)
            nc.scalar.activation(table_warm[:, :], ident[:, 0:1], ACT.Exp).then_inc(zeroed, 1)

            def attention_out(c):
                act.wait_ge(atT_ps, c + 1)
                nc.scalar.activation(atT[:, :, :], bank[:, 0:KT, :], ACT.Copy).then_inc(atT_ready, 1)

            def gate_inputs(c):
                act.wait_ge(xaT_ps, c + 1)
                nc.scalar.activation(xaT[:, :, :], bank[:, 0:KT, :], ACT.Copy).then_inc(xaT_ready, 1)
                act.wait_ge(shifted, c + 1)
                nc.scalar.activation(gates[:, :, :], logits[:, :, :], ACT.Exp).then_inc(exp_done, 1)

            attention_out(0)
            gate_inputs(0)
            with act.Fori(0, NCH) as c:
                for e in range(NE):
                    if e == 2:
                        act.wait_ge(wT_ps, c + 1)
                        nc.scalar.activation(wT[:, :], bank[0:NE, 7, :], ACT.Copy).then_inc(wT_ready, 1)
                    if e >= 2:
                        act.wait_ge(y_ps, c * NE + e - 1)
                    for f in range(FT):
                        act.wait_ge(h_ps, (c * NE + e) * FT + f + 1)
                        nc.scalar.activation(hT[:, e % 2, f, :], bank[:, 2 + f, :], ACT.Relu,
                                             bias=b1[:, e * FT + f:e * FT + f + 1]).then_inc(h_ready, 1)
                    if e == NEXT_AT + 1:
                        attention_out(c + 1)
                gate_inputs(c + 1)

        @block.vector
        def _(dve):
            dve.wait_ge(consts, 2)
            dve.wait_ge(*met)

            def over_tiles(v):
                return v[:, :].rearrange("p (o d) -> p o d", o=1).broadcast_to((P, TT, v.shape[-1]))

            def halves(first):
                return bank[:, first:first + 2, :].rearrange("p b (h d) -> p (b h) d", d=D)

            def block_input(c, n):
                dve.wait_ge(wo_ps, c + 1)
                nc.vector.tensor_tensor(xa[:, :, :], halves(0), over_tiles(rows["bo"]), ALU.add).then_inc(attn_added, 1)
                dve.wait_ge(src_loaded, 16 * (c + 1))
                dve.wait_ge(attn_added, c + 1)
                nc.vector.tensor_tensor(xa[:, :, :], xa[:, :, :], src_in[:, :, :], ALU.add).then_inc(src_used, 1)
                dve.wait_ge(src_used, c + 1)
                layernorm(nc, dve, lambda t: xa[:, t, :], lambda t: xn[:, t, :], stats, mv, ln_sems, n, normal1, c + 1)
                nc.vector.tensor_tensor(xn[:, :, :], xn[:, :, :], over_tiles(rows["ln1_g"]), ALU.mult).then_inc(scaled, 1)
                dve.wait_ge(scaled, c + 1)
                nc.vector.tensor_tensor(xa[:, :, :], xn[:, :, :], over_tiles(rows["ln1_b"]), ALU.add).then_inc(xa_ready, 1)

            def expert_weights(c):
                base = 9 * c
                dve.wait_ge(gates_ps, c + 1)
                pl = bank[:, 0, 0:TT * NE].rearrange("p (t e) -> p t e", e=NE)
                nc.vector.tensor_tensor(logits[:, :, :], pl, over_tiles(gb_rows), ALU.add).then_inc(gate_steps, 1)
                dve.wait_ge(gate_steps, base + 1)
                nc.vector.reduce_max(top[:, :], logits[:, :, :], X).then_inc(gate_steps, 1)
                dve.wait_ge(gate_steps, base + 2)

                def per_token(v):
                    return v[:, :].rearrange("p (t o) -> p t o", o=1).broadcast_to((P, TT, NE))

                nc.vector.tensor_tensor(logits[:, :, :], logits[:, :, :], per_token(top), ALU.subtract).then_inc(shifted, 1)
                dve.wait_ge(exp_done, c + 1)
                nc.vector.reduce_sum(top[:, :], gates[:, :, :], X).then_inc(gate_steps, 1)
                dve.wait_ge(gate_steps, base + 3)
                nc.vector.reciprocal(top[:, :], top[:, :]).then_inc(gate_steps, 1)
                dve.wait_ge(gate_steps, base + 4)
                nc.vector.tensor_tensor(gates[:, :, :], gates[:, :, :], per_token(top), ALU.mult).then_inc(gate_steps, 1)
                dve.wait_ge(gate_steps, base + 5)
                others = [gates[:, :, :].rearrange("p t (o j) -> p t o j", o=1).broadcast_to((P, TT, NE, NE))[:, t, :, :]
                          for t in range(TT)]
                own = [gates[:, :, :].rearrange("p t (e o) -> p t e o", o=1).broadcast_to((P, TT, NE, NE))[:, t, :, :]
                       for t in range(TT)]
                for t in range(TT):
                    nc.vector.tensor_tensor(over[:, t, :, :], others[t], own[t], ALU.is_gt)
                    last = nc.vector.tensor_tensor(ties[:, t, :, :], others[t], own[t], ALU.is_equal)
                last.then_inc(gate_steps, 1)
                dve.wait_ge(gate_steps, base + 6)
                for t in range(TT):
                    last = nc.vector.tensor_tensor(ties[:, t, :, :], ties[:, t, :, :], before[:, :, :], ALU.mult)
                last.then_inc(gate_steps, 1)
                dve.wait_ge(gate_steps, base + 7)
                nc.vector.tensor_tensor(over[:, :, :, :], over[:, :, :, :], ties[:, :, :, :], ALU.add).then_inc(gate_steps, 1)
                dve.wait_ge(gate_steps, base + 8)
                nc.vector.reduce_sum(rank[:, :, :], over[:, :, :, :], X).then_inc(gate_steps, 1)
                dve.wait_ge(gate_steps, base + 9)
                nc.vector.scalar_tensor_tensor(weights[:, :, :], rank[:, :, :], 1.5, gates[:, :, :], ALU.is_lt, ALU.mult
                                               ).then_inc(weights_ready, 1)

            block_input(0, 1)
            expert_weights(0)
            with dve.Fori(0, NCH) as c:
                dve.wait_ge(bias_ps, c + 1)
                nc.vector.tensor_tensor(acc[:, :, :], halves(0), xa[:, :, :], ALU.add).then_inc(added, 1)
                dve.wait_ge(added, 2 * c + 1)
                for e in range(NE):
                    dve.wait_ge(y_ps, c * NE + e + 1)
                    y = halves(6)
                    for t in range(TT):
                        last = nc.vector.scalar_tensor_tensor(acc[:, t, :], y[:, t, :], weights[:, t, e:e + 1], acc[:, t, :],
                                                              ALU.mult, ALU.add)
                    last.then_inc(y_added, 1)
                    dve.wait_ge(y_added, c * NE + e + 2)
                    if e == NEXT_AT + 1:
                        block_input(c + 1, 3 * c + 2)
                expert_weights(c + 1)
                layernorm(nc, dve, lambda t: acc[:, t, :], lambda t: xn[:, t, :], stats, mv, ln_sems, 3 * c + 3, normal2, 2 * c + 1)
                nc.vector.tensor_tensor(xn[:, :, :], xn[:, :, :], over_tiles(rows["ln2_g"]), ALU.mult).then_inc(added, 1)
                dve.wait_ge(added, 2 * c + 2)
                nc.vector.tensor_tensor(acc[:, :, :], xn[:, :, :], over_tiles(rows["ln2_b"]), ALU.add).then_inc(moe_normal, 1)
                dve.wait_ge(moe_normal, c + 1)
                layernorm(nc, dve, lambda t: acc[:, t, :], lambda t: xn[:, t, :], stats, mv, ln_sems, 3 * c + 4, normal2, 2 * c + 2)
                dve.wait_ge(x1_loaded, 16 * (c + 1))
                dve.wait_ge(stored, 16 * (c + 1))
                nc.vector.tensor_tensor(outc[:, :, :], xn[:, :, :], x1_in[:, :, :], ALU.add).then_inc(out_ready, 1)

        @block.tensor
        def _(pe):
            pe.wait_ge(consts, 2)
            pe.wait_ge(*met)

            def transposed(src, done):
                for k in range(KT):
                    for t in range(TT):
                        last = nc.tensor.transpose(bank[:, k, t * P:(t + 1) * P], src[:, t, k * P:(k + 1) * P], ident[:, :])
                last.then_inc(done, 1)

            def by_tokens(first, lhsT, rhs, n, done):
                for t in range(TT):
                    for k in range(n):
                        last = nc.tensor.matmul(bank[:, first + t // 2, (t % 2) * D:(t % 2 + 1) * D], lhsT(k, t), rhs(k),
                                                start=k == 0, stop=k == n - 1)
                last.then_inc(done, 1)

            pe.wait_ge(at_loaded, 16)
            transposed(at_in, atT_ps)
            pe.wait_ge(atT_ready, 1)
            by_tokens(0, lambda k, t: atT[:, k, t * P:(t + 1) * P], lambda k: wo[:, k, :], KT, wo_ps)

            def gate_product(c):
                pe.wait_ge(xaT_ready, c + 1)
                for t in range(TT):
                    for k in range(KT):
                        last = nc.tensor.matmul(bank[:, 0, t * NE:(t + 1) * NE], xaT[:, k, t * P:(t + 1) * P], gw[:, k, :],
                                                start=k == 0, stop=k == KT - 1)
                last.then_inc(gates_ps, 1)

            pe.wait_ge(xa_ready, 1)
            transposed(xa, xaT_ps)
            gate_product(0)
            pe.wait_ge(weights_in, 16 * len(expert_loads))
            with pe.Fori(0, NCH) as c:
                def hidden(e):
                    for f in range(FT):
                        if e:
                            pe.wait_ge(h_ready, (c * NE + e - 1) * FT + f + 1)
                        for k in range(KT):
                            last = nc.tensor.matmul(bank[:, 2 + f, :], w1[:, k, e, f * P:(f + 1) * P], xaT[:, k, :],
                                                    start=k == 0, stop=k == KT - 1)
                        last.then_inc(h_ps, 1)

                hidden(0)
                hidden(1)
                pe.wait_ge(weights_ready, c + 1)
                pe.wait_ge(y_added, c * NE + 1)
                for t in range(TT):
                    last = nc.tensor.transpose(bank[0:NE, 7, t * P:(t + 1) * P], weights[:, t, :], ident[:, :])
                last.then_inc(wT_ps, 1)
                pe.wait_ge(wT_ready, c + 1)
                by_tokens(0, lambda k, t: wT[:, t * P:(t + 1) * P], lambda k: b2[:, :], 1, bias_ps)
                for e in range(NE):
                    if 1 <= e < NE - 1:
                        hidden(e + 1)
                    if e == NEXT_AT:
                        pe.wait_ge(at_loaded, 16 * (c + 2))
                        transposed(at_in, atT_ps)
                    if e == NEXT_AT + 1:
                        pe.wait_ge(atT_ready, c + 2)
                        by_tokens(0, lambda k, t: atT[:, k, t * P:(t + 1) * P], lambda k: wo[:, k, :], KT, wo_ps)
                    if e == NE - 2:
                        pe.wait_ge(xa_ready, c + 2)
                        transposed(xa, xaT_ps)
                    pe.wait_ge(h_ready, (c * NE + e + 1) * FT)
                    pe.wait_ge(y_added, c * NE + e + 1)
                    by_tokens(6, lambda k, t: hT[:, e % 2, k, t * P:(t + 1) * P], lambda k: w2[:, e, k, :], FT, y_ps)
                gate_product(c + 1)


def layouts(z):
    p = {k[len("L0_attn_"):]: np.asarray(v) for k, v in z.items() if k.startswith("L0_attn_")}
    f = {k[len("L0_ffn_"):]: np.asarray(v) for k, v in z.items() if k.startswith("L0_ffn_")}

    def columns(v):
        return v.reshape(-1, P).T

    return {
        "x": p["x"].reshape(T, D),
        "in_w": p["in_proj_w"].T, "xp_w": p["x_proj_w"].T, "dt_w": p["dt_proj_w"].T, "out_w": p["out_proj_w"].T,
        "conv_w": p["conv_w"], "conv_b": columns(p["conv_b"]), "dt_b": columns(p["dt_proj_b"]),
        "log_A": p["log_A"], "Dp": columns(p["Dp"]),
        "norm_g": columns(p["norm_g"]), "norm_b": columns(p["norm_b"]), "bq": columns(f["bq"]), "bk": columns(f["bk"]),
        "b1": f["b1"].reshape(NE * FT, P).T,
        **{k: f[k] for k in ("Wq", "Wk", "Wv", "bv", "Wo", "bo", "gW", "gb", "W1", "W2", "b2",
                             "ln1_g", "ln1_b", "ln2_g", "ln2_b")},
    }


def program(nc, a, out):
    scr = Scratch(nc)
    mamba_stage(nc, a, scr)
    attention_stage(nc, a, scr)
    expert_stage(nc, a, scr, out)


def kernel(**inputs):
    import concourse.bacc as bacc
    from concourse.bass_utils import run_bass_kernel_spmd

    nc = bacc.Bacc("TRN2", target_bir_lowering=False, num_devices=1)
    arrays, args = {}, {}
    for name, value in layouts(inputs).items():
        value = np.ascontiguousarray(value)
        arrays[f"in_{name}"] = value
        args[name] = nc.dram_tensor(f"in_{name}", value.shape, mybir.dt.from_np(value.dtype), kind="ExternalInput").ap()
    out = nc.dram_tensor("out", (T, D), F32, kind="ExternalOutput").ap()
    program(nc, args, out)
    result = run_bass_kernel_spmd(nc, [arrays], core_ids=[0]).results[0]["out"]
    return result.reshape(1, T, D)
```
